# Optimizing a Trainium2 kernel written in Bass

```python
import numpy as np
import jax
import jax.numpy as jnp

def _softmax(x, axis=-1):
    return jax.nn.softmax(x, axis=axis)

def _gelu(x):
    return jax.nn.gelu(x, approximate=True)

def _silu(x):
    return jax.nn.silu(x)

def _sigmoid(x):
    return jax.nn.sigmoid(x)

def _layernorm(x, axis=-1, eps=1e-05):
    m = jnp.mean(x, axis=axis, keepdims=True)
    v = jnp.var(x, axis=axis, keepdims=True)
    return (x - m) / jnp.sqrt(v + eps)

def _scatter_add(tgt, idx, src, axis=0):
    return tgt.at[idx].add(src)

def _segment_sum(src, seg, n):
    return jax.ops.segment_sum(src, seg, n)
kernel_name = 'mk_adj_seq_d2_adj_r2_df67eb'

def setup_inputs(seed: int=0):
    np.random.seed(seed)
    _w = jnp.asarray

    def _rec_inputs():
        import jax
        import jax.numpy as jnp
        _gk = jax.random.key(seed)
        x = -0.000929 + 1 * jax.random.normal(jax.random.fold_in(_gk, 1), (4096, 128), jnp.float32)
        _w = (1.0 + jnp.arange(4096, dtype=jnp.float32)) ** (-0.5)
        _w = _w / _w.mean()
        _pij = jnp.clip(0.00390625 * _w[:, None] * _w[None, :], 0.0, 1.0)
        _a = jax.random.uniform(jax.random.fold_in(_gk, 2), (4096, 4096)) < _pij
        _a = jnp.logical_or(_a, jnp.eye(4096, dtype=bool))
        adj = _a.astype(jnp.int32)
        return (x, adj)
    x, adj = _rec_inputs()

    def _L0_gnn_setup():
        import jax, jax.numpy as jnp
        import numpy as np
        DIM = 128
        HEADS = 8
        DIM_FF = 512
        N = 2048
        HEAD_DIM = DIM // HEADS
        SCALE = HEAD_DIM ** (-0.5)

        def layer_norm(x, gamma, beta, eps=1e-05):
            mu = jnp.mean(x, axis=-1, keepdims=True)
            var = jnp.var(x, axis=-1, keepdims=True)
            return (x - mu) * jax.lax.rsqrt(var + eps) * gamma + beta
        key = jax.random.key(seed)
        ks = jax.random.split(key, 8)
        x = jax.random.normal(ks[0], (N, DIM), dtype=jnp.float32)
        adj = jax.random.randint(ks[1], (N, N), 0, 2, dtype=jnp.int32)
        adj = adj.at[jnp.arange(N), jnp.arange(N)].set(1)
        s = 1.0 / np.sqrt(DIM)
        w_qkv = jax.random.normal(ks[2], (DIM, 3 * DIM), dtype=jnp.float32) * s
        w_proj = jax.random.normal(ks[3], (DIM, DIM), dtype=jnp.float32) * s
        b_proj = jnp.zeros((DIM,), jnp.float32)
        w1 = jax.random.normal(ks[4], (DIM, DIM_FF), dtype=jnp.float32) * s
        b1 = jnp.zeros((DIM_FF,), jnp.float32)
        w2 = jax.random.normal(ks[5], (DIM_FF, DIM), dtype=jnp.float32) / np.sqrt(DIM_FF)
        b2 = jnp.zeros((DIM,), jnp.float32)
        g1 = jnp.ones((DIM,), jnp.float32)
        be1 = jnp.zeros((DIM,), jnp.float32)
        g2 = jnp.ones((DIM,), jnp.float32)
        be2 = jnp.zeros((DIM,), jnp.float32)
        return {'x': x, 'adj': adj, 'w_qkv': w_qkv, 'w_proj': w_proj, 'b_proj': b_proj, 'w1': w1, 'b1': b1, 'w2': w2, 'b2': b2, 'g1': g1, 'be1': be1, 'g2': g2, 'be2': be2}
    _L0_gnn_all = _L0_gnn_setup()
    _L0_gnn_in = {k: v for k, v in _L0_gnn_all.items() if k in ('w_qkv', 'w_proj', 'b_proj', 'w1', 'b1', 'w2', 'b2', 'g1', 'be1', 'g2', 'be2')}
    del _L0_gnn_all

    def _L1_gnn_setup():
        import jax, jax.numpy as jnp
        import numpy as np
        N = 4096
        F = 128
        H = 64
        NEG = -9000000000000000.0
        EPS = 1e-05
        key = jax.random.key(seed)
        ks = jax.random.split(key, 6)
        x = jax.random.normal(ks[0], (N, F), jnp.float32)
        adj = jax.random.randint(ks[1], (N, N), 0, 2, jnp.int32)
        Wt = jax.random.normal(ks[2], (H, F), jnp.float32) * (1.0 / np.sqrt(F))
        bt = jnp.zeros((H,), jnp.float32)
        Wa = jax.random.normal(ks[3], (1, H), jnp.float32) * (1.0 / np.sqrt(H))
        ba = jnp.zeros((1,), jnp.float32)
        Wp = jax.random.normal(ks[4], (F, H), jnp.float32) * (1.0 / np.sqrt(H))
        bp = jnp.zeros((F,), jnp.float32)
        gamma = jnp.ones((F,), jnp.float32)
        beta = jnp.zeros((F,), jnp.float32)
        return dict(x=x, adj=adj, Wt=Wt, bt=bt, Wa=Wa, ba=ba, Wp=Wp, bp=bp, gamma=gamma, beta=beta)
    _L1_gnn_all = _L1_gnn_setup()
    _L1_gnn_in = {k: v for k, v in _L1_gnn_all.items() if k in ('Wt', 'bt', 'Wa', 'ba', 'Wp', 'bp', 'gamma', 'beta')}
    del _L1_gnn_all
    return {'x': x, 'adj': adj, 'L0_gnn_w_qkv': _L0_gnn_in['w_qkv'], 'L0_gnn_w_proj': _L0_gnn_in['w_proj'], 'L0_gnn_b_proj': _L0_gnn_in['b_proj'], 'L0_gnn_w1': _L0_gnn_in['w1'], 'L0_gnn_b1': _L0_gnn_in['b1'], 'L0_gnn_w2': _L0_gnn_in['w2'], 'L0_gnn_b2': _L0_gnn_in['b2'], 'L0_gnn_g1': _L0_gnn_in['g1'], 'L0_gnn_be1': _L0_gnn_in['be1'], 'L0_gnn_g2': _L0_gnn_in['g2'], 'L0_gnn_be2': _L0_gnn_in['be2'], 'L1_gnn_Wt': _L1_gnn_in['Wt'], 'L1_gnn_bt': _L1_gnn_in['bt'], 'L1_gnn_Wa': _L1_gnn_in['Wa'], 'L1_gnn_ba': _L1_gnn_in['ba'], 'L1_gnn_Wp': _L1_gnn_in['Wp'], 'L1_gnn_bp': _L1_gnn_in['bp'], 'L1_gnn_gamma': _L1_gnn_in['gamma'], 'L1_gnn_beta': _L1_gnn_in['beta']}

def reference(x, adj, L0_gnn_w_qkv, L0_gnn_w_proj, L0_gnn_b_proj, L0_gnn_w1, L0_gnn_b1, L0_gnn_w2, L0_gnn_b2, L0_gnn_g1, L0_gnn_be1, L0_gnn_g2, L0_gnn_be2, L1_gnn_Wt, L1_gnn_bt, L1_gnn_Wa, L1_gnn_ba, L1_gnn_Wp, L1_gnn_bp, L1_gnn_gamma, L1_gnn_beta):
    import jax
    import jax.numpy as jnp

    def _L0_gnn_ref(x, adj, w_qkv, w_proj, b_proj, w1, b1, w2, b2, g1, be1, g2, be2):
        import jax, jax.numpy as jnp
        import numpy as np
        DIM = 128
        HEADS = 8
        DIM_FF = 512
        N = 2048
        HEAD_DIM = DIM // HEADS
        SCALE = HEAD_DIM ** (-0.5)

        def layer_norm(x, gamma, beta, eps=1e-05):
            mu = jnp.mean(x, axis=-1, keepdims=True)
            var = jnp.var(x, axis=-1, keepdims=True)
            return (x - mu) * jax.lax.rsqrt(var + eps) * gamma + beta
        n = x.shape[0]
        qkv = layer_norm(x, g1, be1) @ w_qkv
        qkv = qkv.reshape(n, 3, HEADS, HEAD_DIM)
        q, k, v = (qkv[:, 0], qkv[:, 1], qkv[:, 2])
        scores = jnp.einsum('nhd,mhd->hnm', q, k) * SCALE
        mask = (adj != 0)[None, :, :]
        scores = jnp.where(mask, scores, -jnp.inf)
        attn = jax.nn.softmax(scores, axis=-1)
        out = jnp.einsum('hnm,mhd->nhd', attn, v).reshape(n, DIM)
        x = x + out @ w_proj + b_proj
        h2 = layer_norm(x, g2, be2)
        ff = jax.nn.gelu(h2 @ w1 + b1) @ w2 + b2
        return x + ff

    def _L1_gnn_ref(x, adj, Wt, bt, Wa, ba, Wp, bp, gamma, beta):
        import jax, jax.numpy as jnp
        import numpy as np
        N = 4096
        F = 128
        H = 64
        NEG = -9000000000000000.0
        EPS = 1e-05
        h = x @ Wt.T + bt
        s = jax.nn.leaky_relu(h @ Wa.T + ba, negative_slope=0.2)
        scores = jnp.where(adj > 0, s, jnp.float32(NEG))
        w = jax.nn.softmax(scores, axis=1)
        neighbor = w @ h
        tf = neighbor @ Wp.T + bp
        y = x + tf
        mu = jnp.mean(y, axis=-1, keepdims=True)
        var = jnp.var(y, axis=-1, keepdims=True)
        return gamma * (y - mu) * jax.lax.rsqrt(var + EPS) + beta
    x = _L0_gnn_ref(x, adj, L0_gnn_w_qkv, L0_gnn_w_proj, L0_gnn_b_proj, L0_gnn_w1, L0_gnn_b1, L0_gnn_w2, L0_gnn_b2, L0_gnn_g1, L0_gnn_be1, L0_gnn_g2, L0_gnn_be2)
    x = _L1_gnn_ref(x, adj, L1_gnn_Wt, L1_gnn_bt, L1_gnn_Wa, L1_gnn_ba, L1_gnn_Wp, L1_gnn_bp, L1_gnn_gamma, L1_gnn_beta)
    return x

_drawn_inputs = setup_inputs


def setup_inputs(seed=0):
    import zlib

    import numpy as np

    out = dict(_drawn_inputs(seed))
    spreads = {'L0_gnn_b_proj': (0.0, 0.1),
     'L0_gnn_b1': (0.0, 0.1),
     'L0_gnn_b2': (0.0, 0.1),
     'L0_gnn_g1': (1.0, 0.2),
     'L0_gnn_be1': (0.0, 0.1),
     'L0_gnn_g2': (1.0, 0.2),
     'L0_gnn_be2': (0.0, 0.1),
     'L1_gnn_bt': (0.0, 0.1),
     'L1_gnn_bp': (0.0, 0.1),
     'L1_gnn_gamma': (1.0, 0.2),
     'L1_gnn_beta': (0.0, 0.1)}
    factors = {}
    for name, (base, spread) in spreads.items():
        noise = np.random.default_rng([zlib.crc32(name.encode()), seed]).standard_normal(out[name].shape)
        drawn = base * np.exp(spread * noise) if base else spread * noise
        out[name] = jnp.asarray(drawn.astype(out[name].dtype))
    for name, factor in factors.items():
        out[name] = (out[name] * factor).astype(out[name].dtype)
    return out
```

```python
from contextlib import ExitStack

import concourse.bass as bass
from concourse import mybir

F32 = mybir.dt.float32
BF16 = mybir.dt.bfloat16
I32 = mybir.dt.int32
ALU = mybir.AluOpType
ACT = mybir.ActivationFunctionType
AX = mybir.AxisListType
ds = bass.ds

P = 128
D = 128
H, HD = 8, 16
HG = H // 2
CH = 512
SUB = CH // P
PARTS = 6 * HD
KW = PARTS + 3
PACK = 100
VW = HD + 1
SLOTS = 4
RING = 4
LEAD = 3
FF = 512
HID = 64
HUGE = 2.0 ** 127
NEG = -9000000000000000.0
SAFE = 38.0
EPS = 1e-5


def gnn_kernel(nc, x, adj, w_qkv, w_proj, b_proj, w1, b1, w2, b2, g1, be1, g2, be2,
               Wt, bt, Wa, ba, Wp, bp, gamma, beta, out):
    N = x.shape[0]
    NT, NC = N // P, N // CH
    NB = NT // SLOTS
    MB = NT // 2
    SEG_UNITS = 2 * NT
    SCALE = float(HD) ** -0.5

    q_dram = nc.dram_tensor("q_packed", (NT, KW, H, P), BF16).ap()
    v_dram = nc.dram_tensor("v_ones", (2, NT, P, HG * VW), F32).ap()
    m_dram = nc.dram_tensor("mask_t", (NC, P, NT, CH), BF16).ap()
    a_dram = nc.dram_tensor("attn_t", (NC, P, 2, CH), F32).ap()

    with ExitStack() as ctx:
        def sb(name, shape, dt):
            return ctx.enter_context(nc.sbuf_tensor(name, shape, dt))

        def sem(name):
            return ctx.enter_context(nc.semaphore(name))

        k_pack = sb("k_pack", [P, max(H * N, 32768)], BF16)
        mask_t = sb("mask_t_sb", [P, max(2 * NT * CH, 32768)], BF16)
        q_pack = sb("q_pack", [P, 2, HG, CH], BF16)
        probs = sb("probs", [P, SLOTS, 2, 2 * CH], F32)
        v_st = sb("v_st", [P, SLOTS, HG * VW], F32)
        adj_in = sb("adj_in", [P, SUB, 2 * P], I32)
        mask_n = sb("mask_n", [P, SUB, 2 * P], BF16)
        acc_sb = sb("acc_sb", [P, 2, CH], F32)
        ident = sb("ident", [P, P], BF16)
        identf = sb("identf", [P, P], F32)
        ones_b = sb("ones_b", [P, P], BF16)
        zeros = sb("zeros", [1, CH], BF16)
        cols = sb("cols", [P, 16], F32)
        small = sb("small", [P, 8, 16], F32)
        flag = sb("flag", [P, 2], I32)
        ps = ctx.enter_context(nc.psum_tensor("ps", [P, 8, CH], F32))

        m_view = mask_t[:, 0:2 * NT * CH].rearrange("p (s t q) -> p s t q", s=2, t=NT)
        k_view = k_pack[:, 0:H * N].rearrange("p (h n) -> p h n", h=H)
        bank16 = [ps[:, b, :].bitcast(BF16) for b in range(8)]

        x_sb = mask_t[:, NT * CH:].bitcast(F32)[:, 0:NT * D].rearrange("p (t d) -> p t d", d=D)
        stat_area = mask_t[:, NT * CH:].bitcast(F32)[:, NT * D:]
        taken = [0]

        def stat(n):
            taken[0] += n
            return stat_area[:, taken[0] - n:taken[0]]
        bn = stat(6 * NT).rearrange("p (t k) -> p t k", k=6)
        mv = stat(2 * NT).rearrange("p (t k) -> p t k", k=2)
        rstd = stat(NT)
        norms = stat(16 * NT).rearrange("p (t k) -> p t k", k=16)
        pool_words = probs[:, :, :, :].rearrange("p a b c -> p (a b c)")
        used = [0]

        def part(n):
            used[0] += n
            return pool_words[:, used[0] - n:used[0]]
        packed = part(RING * 16 * PACK // 2).bitcast(BF16).rearrange("p (u h k) -> p u h k", u=RING, h=16)
        r1 = part(512).rearrange("p (u n) -> p u n", u=2)
        sq = part(512).rearrange("p (u n) -> p u n", u=2)
        xn = part(256).rearrange("p (u n) -> p u n", u=2)
        hT = part(RING * P).rearrange("p (u n) -> p u n", u=RING)
        v_out = part(RING * H * VW).rearrange("p (u h k) -> p u h k", u=RING, h=H)
        q_out = part(RING * H * P // 2).bitcast(BF16).rearrange("p (u h q) -> p u h q", u=RING, h=H)
        wqkv = part(3 * D)

        phase = sem("phase")
        settled = sem("settled")
        params_in = sem("params_in")
        x_in = [sem(f"x_in{j}") for j in range(4)]
        w_scaled = sem("w_scaled")
        const_made = sem("const_made")
        ident_zeroed = sem("ident_zeroed")
        bn_made = sem("bn_made")
        var_made = sem("var_made")
        eps_added = sem("eps_added")
        rstd_made = sem("rstd_made")
        xn_made = sem("xn_made")
        xT_done = sem("xT_done")
        hT_made = sem("hT_made")
        qkv_done = sem("qkv_done")
        hi_made = sem("hi_made")
        r1_made = sem("r1_made")
        mid_made = sem("mid_made")
        lo_made = sem("lo_made")
        sq_made = sem("sq_made")
        norms_made = sem("norms_made")
        nT_done = sem("nT_done")
        q_out_made = sem("q_out_made")
        k_made = sem("k_made")
        q_stored = [sem(f"q_stored{u}") for u in range(RING)]
        v_stored = [sem(f"v_stored{u}") for u in range(RING)]
        bound_step = sem("bound_step")
        flag_made = sem("flag_made")
        adj_loaded = sem("adj_loaded")
        converted = sem("converted")
        turned = sem("turned")
        evacuated = sem("evacuated")
        mask_stored = sem("mask_stored")
        q_loaded = [sem("q_loaded0"), sem("q_loaded1")]
        v_loaded = [sem("v_loaded0"), sem("v_loaded1")]
        scored = sem("scored")
        exped = sem("exped")
        masked = sem("masked")
        pv_done = sem("pv_done")
        acc_copied = [sem("acc_copied0"), sem("acc_copied1")]
        acc_stored = [sem("acc_stored0"), sem("acc_stored1")]

        XN, TP, SB2, ONE = 2, 2, 2, 1

        t_words = mask_t[:, :].bitcast(F32)
        w_words = k_pack[:, :].bitcast(F32)
        t_used, w_used = [0], [0]

        def tb(*shape):
            n = 1
            for s in shape:
                n *= s
            t_used[0] += n
            assert t_used[0] <= t_words.shape[1]
            v = t_words[:, t_used[0] - n:t_used[0]]
            return v.rearrange("p (a b) -> p a b", b=shape[-1]) if len(shape) > 1 else v

        def wb(*shape):
            n = 1
            for s in shape:
                n *= s
            w_used[0] += n
            assert w_used[0] <= w_words.shape[1]
            v = w_words[:, w_used[0] - n:w_used[0]]
            return v.rearrange("p (a b) -> p a b", b=shape[-1]) if len(shape) > 1 else v

        x2_sb = wb(NT, D)
        h3 = wb(NT * 98).bitcast(BF16).rearrange("p (t k) -> p t k", k=196)
        s_row = wb(NT)
        w1_sb, w2_sb, wp_sb = wb(FF), wb(FF // P, D), wb(D)
        wtT, wpT = wb(HID), wb(D)
        wt_raw, wpr_raw = wb(D), wb(HID)
        bproj_r, b2_r, bp_r, gamma_r, beta_r = wb(D), wb(D), wb(D), wb(D), wb(D)
        bt_r, wa_r, ba_r, csum = wb(HID), wb(HID), wb(1), wb(HID)
        b1_c, g2_c, be2_c = wb(FF // P), wb(1), wb(1)
        e1, e0, mx = wb(NT), wb(NT), wb(NT)

        class Half:
            pass
        halves = []
        for u in range(2):
            f = Half()
            f.acc, f.x, f.xb = tb(2, CH), tb(SUB, D), tb(SUB, D)
            f.att, f.attT, f.x1 = tb(SUB * H, HD), tb(CH), tb(SUB, D)
            f.bn, f.mv, f.rl, f.rstd = tb(SUB, 6), tb(SUB, 2), tb(2 * SUB * HG), tb(SUB)
            f.h2, f.h2T = tb(SUB, D), tb(CH)
            f.ff = pool_words[:, 2048 * u:2048 * u + 2048].rearrange("p (m q) -> p m q", q=CH)
            f.x2 = tb(SUB, D)
            f.x1b, f.x2T, f.h, f.r = tb(SUB, D), tb(CH), tb(SUB, HID), tb(SUB, HID)
            f.banks = [4 * u + k for k in range(4)]
            halves.append(f)

        tail_in = sem("tail_in")
        ones_made = sem("ones_made")
        wT_turned, wT_copied = sem("wT_turned"), sem("wT_copied")
        acc_in = [sem("acc_in0"), sem("acc_in1")]
        pe_step = [sem("pe_step0"), sem("pe_step1")]
        act_step = [sem("act_step0"), sem("act_step1")]
        dve_step = [sem("dve_step0"), sem("dve_step1")]
        pool_step = [sem("pool_step0"), sem("pool_step1")]
        (P_ACC, P_ATT, P_PROJ, P_H, P_FF1, _, _, P_FF, P_OUT, P_X2, P_HID), PE_N = range(1, 12), 11
        (A_ATT, A_H, A_G1, _, _, A_G, A_X2), ACT_N = range(1, 8), 7
        (V_RL, V_ATT, V_X1, V_BN, V_AG, V_H2, V_X2, V_HID, V_HI, V_R1, V_MID, V_LO, V_SP, V_S, V_SB,
         V_LR), DVE_N = range(1, 17), 16
        (G_XB, G_EPS, G_RSTD, G_X1B, G_X2), POOL_N = range(1, 6), 5

        def steps(sems, u, number, j):
            return lambda s: (sems[u], number * j + s + 1)

        NP2 = NC // 2

        def tail_sync(sp):
            def load(dst, src, s=tail_in):
                sp.dma_start(dst, src).then_inc(s, 16)
            load(w1_sb, w1)
            load(w2_sb[:, :, :], w2.rearrange("(m p) d -> p m d", p=P))
            load(wp_sb, w_proj)
            load(wt_raw[0:HID, :], Wt)
            load(wpr_raw, Wp)
            for r, v in ((bproj_r, b_proj), (b2_r, b2), (bp_r, bp), (gamma_r, gamma), (beta_r, beta),
                         (bt_r, bt), (wa_r, Wa.rearrange("a b -> (a b)")), (ba_r, ba)):
                load(r, v.rearrange("(a n) -> a n", a=1).to_broadcast([P, v.shape[0]]))
            for m in range(FF // P):
                load(b1_c[:, m:m + 1], b1[m * P:(m + 1) * P].rearrange("(p a) -> p a", a=1))
            load(g2_c, g2.rearrange("(p a) -> p a", a=1))
            load(be2_c, be2.rearrange("(p a) -> p a", a=1))

            with sp.Fori(0, NP2) as j:
                for u, f in enumerate(halves):
                    c = 2 * j + u
                    if True:
                        sp.wait_ge(dve_step[u], DVE_N * j + 1)
                        sp.wait_ge(pe_step[u], PE_N * j + 1)
                        sp.wait_ge(pool_step[u], POOL_N * j + 1)
                    sp.dma_start(f.acc[:, :, :], a_dram[c, :, :, :]).then_inc(acc_in[u], 16)
                    sp.dma_start(f.x[:, :, :], x[ds(c * CH, CH), :].rearrange("(s p) d -> p s d", p=P))\
                        .then_inc(acc_in[u], 16)
            phase_end(sp, 3)
            layer2_sync(sp)

        N_TAIL_IN = 16 * (15 + FF // P)

        def tail_gpsimd(pool):
            for u in range(2):
                pool.sem_inc(pool_step[u], 1)
            pool.wait_ge(tail_in, N_TAIL_IN)
            nc.gpsimd.memset(h3[:, :, 3 * HID:], 1.0)
            with pool.Fori(0, NP2) as j:
                for u, f in enumerate(halves):
                    pool.wait_ge(acc_in[u], 32 * j + 32)
                    rb = bproj_r.rearrange("p (a d) -> p a d", a=1).to_broadcast([P, SUB, D])
                    nc.gpsimd.tensor_tensor(f.xb, f.x, rb, ALU.add).then_inc(pool_step[u], 1)
                for u, f in enumerate(halves):
                    pool.wait_ge(dve_step[u], DVE_N * j + V_AG + 1)
                    nc.gpsimd.tensor_tensor(f.rstd, f.mv[:, :, 1], cols[:, 9:10].to_broadcast([P, SUB]), ALU.add).then_inc(pool_step[u], 1)
                    pool.wait_ge(pool_step[u], POOL_N * j + G_EPS + 1)
                    nc.gpsimd.tensor_tensor(f.rstd, f.rstd, cols[:, 8:9].to_broadcast([P, SUB]), ALU.pow)\
                        .then_inc(pool_step[u], 1)
                    rb = b2_r.rearrange("p (a d) -> p a d", a=1).to_broadcast([P, SUB, D])
                    nc.gpsimd.tensor_tensor(f.x1b, f.x1, rb, ALU.add).then_inc(pool_step[u], 1)
                for u, f in enumerate(halves):
                    pool.wait_ge(dve_step[u], DVE_N * j + V_X2 + 1)
                    rb = bp_r.rearrange("p (a d) -> p a d", a=1).to_broadcast([P, SUB, D])
                    nc.gpsimd.tensor_tensor(x2_sb[:, ds((2 * j + u) * SUB, SUB), :], f.x2, rb, ALU.add)\
                        .then_inc(pool_step[u], 1)
            phase_end(pool, 3)
            layer2_gpsimd(pool)

        def tail_scalar(act):
            for u in range(2):
                act.sem_inc(act_step[u], 1)
            act.wait_ge(tail_in, N_TAIL_IN)
            act.wait_ge(wT_turned, 1)
            nc.scalar.activation(wtT, ps[:, 0, 0:HID], ACT.Copy)
            nc.scalar.activation(wpT[0:HID, :], ps[0:HID, 1, 0:D], ACT.Copy).then_inc(wT_copied, 1)
            with act.Fori(0, NP2) as j:
                def pe_at(u, s):
                    act.wait_ge(pe_step[u], PE_N * j + s + 1)
                for u, f in enumerate(halves):
                    pe_at(u, P_ATT)
                    nc.scalar.activation(f.attT, ps[:, f.banks[2], :], ACT.Copy).then_inc(act_step[u], 1)
                for u, f in enumerate(halves):
                    pe_at(u, P_H)
                    nc.scalar.activation(f.h2T, ps[:, f.banks[2], :], ACT.Identity, bias=be2_c, scale=g2_c)\
                        .then_inc(act_step[u], 1)
                for u, f in enumerate(halves):
                    for m in range(FF // P):
                        pe_at(u, P_FF1 + m)
                        nc.scalar.activation(f.ff[:, m, :], ps[:, f.banks[m], :], ACT.Gelu_apprx_tanh,
                                             bias=b1_c[:, m:m + 1]).then_inc(act_step[u], 1)
                for u, f in enumerate(halves):
                    pe_at(u, P_X2)
                    nc.scalar.activation(f.x2T, ps[:, f.banks[1], :], ACT.Copy).then_inc(act_step[u], 1)
            phase_end(act, 3)
            layer2_scalar(act)

        def tail_vector(dve):
            for u in range(2):
                dve.sem_inc(dve_step[u], 1)
            dve.wait_ge(tail_in, N_TAIL_IN)
            with dve.Fori(0, NP2) as j:
                def pe_at(u, s):
                    dve.wait_ge(pe_step[u], PE_N * j + s + 1)

                def own(u, s):
                    dve.wait_ge(dve_step[u], DVE_N * j + s + 1)

                def pool_at(u, s):
                    dve.wait_ge(pool_step[u], POOL_N * j + s + 1)

                for u, f in enumerate(halves):
                    t = ps[:, f.banks[0]:f.banks[0] + 2, :].rearrange("p g (s h k) -> p g s h k", s=SUB, h=HG)
                    rl = f.rl.rearrange("p (g s h) -> p g s h", g=2, s=SUB)
                    pe_at(u, P_ACC)
                    nc.vector.reciprocal(f.rl.rearrange("p (a h) -> p a h", h=HG), t[:, :, :, :, HD].rearrange("p g s h -> p (g s) h"))\
                        .then_inc(dve_step[u], 1)
                    own(u, V_RL)
                    att = f.att.rearrange("p (s g h) d -> p g s h d", s=SUB, g=2)
                    for g in range(2):
                        last = nc.vector.tensor_tensor(
                            att[:, g, :, :, :], t[:, g, :, :, 0:HD],
                            rl[:, g, :, :].rearrange("p s (h a) -> p s h a", a=1).to_broadcast([P, SUB, HG, HD]),
                            ALU.mult)
                    last.then_inc(dve_step[u], 1)
                for u, f in enumerate(halves):
                    pe_at(u, P_PROJ)
                    pool_at(u, G_XB)
                    nc.vector.tensor_tensor(f.x1, ps[:, f.banks[3], :].rearrange("p (s d) -> p s d", s=SUB),
                                            f.xb, ALU.add).then_inc(dve_step[u], 1)
                    own(u, V_X1)
                    for s in range(SUB):
                        last = nc.vector.bn_stats(f.bn[:, s, :], f.x1[:, s, :])
                    last.then_inc(dve_step[u], 1)
                    own(u, V_BN)
                    settle(dve)
                    for s in range(SUB):
                        last = nc.vector.bn_aggr(f.mv[:, s, :], f.bn[:, s, :])
                    last.then_inc(dve_step[u], 1)
                for u, f in enumerate(halves):
                    pool_at(u, G_RSTD)
                    for s in range(SUB):
                        last = nc.vector.tensor_scalar(f.h2[:, s, :], f.x1[:, s, :], f.mv[:, s, 0:1],
                                                       f.rstd[:, s:s + 1], ALU.subtract, ALU.mult)
                    last.then_inc(dve_step[u], 1)
                for u, f in enumerate(halves):
                    pe_at(u, P_OUT)
                    pool_at(u, G_X1B)
                    nc.vector.tensor_tensor(f.x2, ps[:, f.banks[0], :].rearrange("p (s d) -> p s d", s=SUB),
                                            f.x1b, ALU.add).then_inc(dve_step[u], 1)
                for u, f in enumerate(halves):
                    at = ds((2 * j + u) * SUB, SUB)
                    pe_at(u, P_HID)
                    nc.vector.tensor_tensor(f.h, ps[:, f.banks[2], 0:SUB * HID].rearrange("p (s d) -> p s d", s=SUB),
                                            bt_r.rearrange("p (a d) -> p a d", a=1).to_broadcast([P, SUB, HID]),
                                            ALU.add).then_inc(dve_step[u], 1)
                    own(u, V_HID)
                    nc.vector.tensor_copy(h3[:, at, 0:HID], f.h).then_inc(dve_step[u], 1)
                    own(u, V_HI)
                    nc.vector.tensor_tensor(f.r, f.h, h3[:, at, 0:HID], ALU.subtract).then_inc(dve_step[u], 1)
                    own(u, V_R1)
                    nc.vector.tensor_copy(h3[:, at, HID:2 * HID], f.r).then_inc(dve_step[u], 1)
                    own(u, V_MID)
                    nc.vector.tensor_tensor(h3[:, at, 2 * HID:3 * HID], f.r, h3[:, at, HID:2 * HID],
                                            ALU.subtract).then_inc(dve_step[u], 1)
                    own(u, V_LO)
                    nc.vector.tensor_tensor(f.r, f.h, wa_r.rearrange("p (a d) -> p a d", a=1)
                                            .to_broadcast([P, SUB, HID]), ALU.mult).then_inc(dve_step[u], 1)
                    own(u, V_SP)
                    nc.vector.tensor_reduce(s_row[:, at], f.r, AX.X, ALU.add).then_inc(dve_step[u], 1)
                    own(u, V_S)
                    nc.vector.tensor_scalar(s_row[:, at], s_row[:, at], ba_r, None, ALU.add).then_inc(dve_step[u], 1)
                    own(u, V_SB)
                    nc.vector.scalar_tensor_tensor(out=s_row[:, at], in0=s_row[:, at], scalar=0.2,
                                                   in1=s_row[:, at], op0=ALU.mult, op1=ALU.max)\
                        .then_inc(dve_step[u], 1)
            phase_end(dve, 3)
            layer2_vector(dve)

        def tail_tensor(pe):
            for u in range(2):
                pe.sem_inc(pe_step[u], 1)
            pe.wait_ge(tail_in, N_TAIL_IN)
            nc.tensor.transpose(ps[:, 0, 0:HID], wt_raw[0:HID, :], identf[0:HID, 0:HID])
            nc.tensor.transpose(ps[0:HID, 1, 0:D], wpr_raw, identf[:, :]).then_inc(wT_turned, 1)
            pe.wait_ge(wT_copied, 1)
            with pe.Fori(0, NP2) as j:
                def act_at(u, s):
                    pe.wait_ge(act_step[u], ACT_N * j + s + 1)

                def dve_at(u, s):
                    pe.wait_ge(dve_step[u], DVE_N * j + s + 1)

                for u, f in enumerate(halves):
                    pe.wait_ge(acc_in[u], 32 * j + 32)
                    dve_at(u, 0)
                    for g in range(2):
                        for s in range(SUB):
                            last = nc.tensor.transpose(ps[:, f.banks[g], s * P:(s + 1) * P],
                                                       f.acc[:, g, s * P:(s + 1) * P], identf[:, :])
                    last.then_inc(pe_step[u], 1)
                for u, f in enumerate(halves):
                    dve_at(u, V_ATT)
                    for s in range(SUB):
                        last = nc.tensor.transpose(ps[:, f.banks[2], s * P:(s + 1) * P],
                                                   f.att[:, s * H:(s + 1) * H, :].rearrange("p h d -> p (h d)"),
                                                   identf[:, :])
                    last.then_inc(pe_step[u], 1)
                for u, f in enumerate(halves):
                    act_at(u, A_ATT)
                    for s in range(SUB):
                        last = nc.tensor.matmul(ps[:, f.banks[3], s * D:(s + 1) * D],
                                                f.attT[:, s * P:(s + 1) * P], wp_sb, start=True, stop=True)
                    last.then_inc(pe_step[u], 1)
                for u, f in enumerate(halves):
                    dve_at(u, V_H2)
                    for s in range(SUB):
                        last = nc.tensor.transpose(ps[:, f.banks[2], s * P:(s + 1) * P], f.h2[:, s, :],
                                                   identf[:, :])
                    last.then_inc(pe_step[u], 1)
                for u, f in enumerate(halves):
                    act_at(u, A_H)
                    for m in range(FF // P):
                        nc.tensor.matmul(ps[:, f.banks[m], :], w1_sb[:, m * P:(m + 1) * P], f.h2T,
                                         start=True, stop=True).then_inc(pe_step[u], 1)
                for u, f in enumerate(halves):
                    act_at(u, A_G)
                    for s in range(SUB):
                        for m in range(FF // P):
                            last = nc.tensor.matmul(ps[:, f.banks[0], s * D:(s + 1) * D],
                                                    f.ff[:, m, s * P:(s + 1) * P], w2_sb[:, m, :],
                                                    start=m == 0, stop=m == FF // P - 1)
                    last.then_inc(pe_step[u], 1)
                for u, f in enumerate(halves):
                    dve_at(u, V_X2)
                    for s in range(SUB):
                        last = nc.tensor.transpose(ps[:, f.banks[1], s * P:(s + 1) * P], f.x2[:, s, :],
                                                   identf[:, :])
                    last.then_inc(pe_step[u], 1)
                for u, f in enumerate(halves):
                    act_at(u, A_X2)
                    for s in range(SUB):
                        last = nc.tensor.matmul(ps[:, f.banks[2], s * HID:(s + 1) * HID],
                                                f.x2T[:, s * P:(s + 1) * P], wtT, start=True, stop=True)
                    last.then_inc(pe_step[u], 1)
            phase_end(pe, 3)
            layer2_tensor(pe)

        KB = 8
        NK = NT // KB
        edges = [pool_words[:, 2048 * r:2048 * (r + 1)].bitcast(BF16).rearrange("p (t q) -> p t q", q=CH)
                 for r in range(2)]
        AGG = 3 * HID + 1
        rest = [4096]

        def lb(*shape):
            n = 1
            for s in shape:
                n *= s
            rest[0] += n
            v = pool_words[:, rest[0] - n:rest[0]]
            return v.rearrange("p (a b) -> p a b", b=shape[-1]) if len(shape) > 1 else v
        nlo, nsum, den, aw, ew = lb(SUB, HID), lb(SUB, HID), lb(SUB), lb(SUB), lb(SUB)
        wc, nbT, y = lb(SUB, HID), lb(CH), lb(SUB, D)
        ybn, ymv, yrs = lb(SUB, 6), lb(SUB, 2), lb(SUB)

        edges_in = [sem("edges_in0"), sem("edges_in1")]
        edges_made = sem("edges_made")
        edges_used = sem("edges_used")
        ones_done = sem("ones_done")
        row_step = sem("row_step")
        e_made = sem("e_made")
        lo_copied = sem("lo_copied")
        agg_read = sem("agg_read")
        den_step = sem("den_step")
        nb_made = sem("nb_made")
        nb_turned = sem("nb_turned")
        nbT_made = sem("nbT_made")
        y_done = sem("y_done")
        y_step = sem("y_step")
        yr_step = sem("yr_step")
        y_normed = sem("y_normed")
        out_made = sem("out_made")
        out_stored = sem("out_stored")

        def layer2_sync(sp):
            sp.sem_inc(out_stored, 16)

            def loads(c):
                for kb in range(NK):
                    BL = c * NK + kb
                    r = kb % 2 if NK > 1 else 0
                    sp.wait_ge(edges_used, BL + 1)
                    sp.dma_start(edges[r][:, :, :], m_dram[c, :, kb * KB:(kb + 1) * KB, :])\
                        .then_inc(edges_in[r], 16)

            def store(c):
                sp.wait_ge(out_made, c + 1)
                o = out[ds(c * CH, CH), :].rearrange("(s p) d -> p s d", p=P)
                sp.dma_start(o, y[:, :, :]).then_inc(out_stored, 16)

            loads(0)
            with sp.Fori(1, NC) as c:
                loads(c)
                store(c - 1)
            store(NC - 1)
            sp.wait_ge(out_stored, 16 * (NC + 1))

        ES = 2 if NK > 1 else 1

        def layer2_gpsimd(pool):
            with pool.Fori(0, NC) as c:
                pool.wait_ge(y_step, 3 * c + 3 + 1)
                nc.gpsimd.tensor_tensor(yrs, ymv[:, :, 1], cols[:, 9:10].to_broadcast([P, SUB]), ALU.add).then_inc(yr_step, 1)
                pool.wait_ge(yr_step, 2 * c + 1)
                nc.gpsimd.tensor_tensor(yrs, yrs, cols[:, 8:9].to_broadcast([P, SUB]), ALU.pow)\
                    .then_inc(yr_step, 1)

        def layer2_scalar(act):
            act.wait_ge(row_step, 3)
            nc.scalar.activation(e1, e1, ACT.Exp)
            nc.scalar.activation(e0, e0, ACT.Exp).then_inc(e_made, 1)

            def parts(c):
                act.wait_ge(edges_used, (c + 1) * NK + ES)
                act.wait_ge(agg_read, c + 1)
                nc.scalar.activation(nlo, ps[:, 0:SUB, 2 * HID:3 * HID], ACT.Copy).then_inc(lo_copied, 1)

            def turned_nb(c):
                act.wait_ge(nb_turned, c + 1 + 1)
                act.wait_ge(y_done, c + 1)
                nc.scalar.activation(nbT[0:HID, :], ps[0:HID, 4, :], ACT.Copy).then_inc(nbT_made, 1)

            parts(0)
            with act.Fori(1, NC) as c:
                turned_nb(c - 1)
                parts(c)
            turned_nb(NC - 1)

        def layer2_vector(dve):
            for s in (agg_read, nb_made, y_step):
                dve.sem_inc(s, 1)
            dve.wait_ge(ones_done, 1)
            nc.vector.tensor_copy(csum, ps[:, 5, 2 * HID:3 * HID]).then_inc(row_step, 1)
            nc.vector.tensor_scalar(mx, s_row, NEG, None, ALU.max).then_inc(row_step, 1)
            dve.wait_ge(row_step, 2)
            nc.vector.tensor_tensor(csum, csum, ps[:, 5, HID:2 * HID], ALU.add)
            nc.vector.tensor_tensor(e1, s_row, mx, ALU.subtract)
            nc.vector.tensor_scalar(e0, mx, -1.0, NEG, ALU.mult, ALU.add).then_inc(row_step, 1)
            dve.wait_ge(row_step, 3)
            nc.vector.tensor_tensor(csum, csum, ps[:, 5, 0:HID], ALU.add).then_inc(row_step, 1)
            dve.wait_ge(e_made, 1)
            nc.vector.tensor_tensor(e1, e1, e0, ALU.subtract).then_inc(row_step, 1)
            dve.wait_ge(row_step, 5)

            def edge_blocks(c, kbs):
                for kb in kbs:
                    r = kb % 2 if NK > 1 else 0
                    BL = c * NK + kb
                    n = (c * NK // 2 + kb // 2) if NK > 1 else c
                    dve.wait_ge(edges_in[r], 16 * n + 16)
                    nc.vector.tensor_scalar(edges[r][:, :, :], edges[r][:, :, :], 0.0, None, ALU.is_ge)\
                        .then_inc(edges_made, 1)

            def read_agg(c):
                dve.wait_ge(lo_copied, c + 1)
                dve.wait_ge(nb_turned, c + 1)
                nc.vector.tensor_tensor(nsum, ps[:, 0:SUB, HID:2 * HID], nlo, ALU.add)
                nc.vector.tensor_tensor(den, ps[:, 0:SUB, 3 * HID], e1[:, ds(c * SUB, SUB)], ALU.mult)\
                    .then_inc(den_step, 1)
                dve.wait_ge(den_step, 4 * c + 1)
                nc.vector.tensor_tensor(nsum, ps[:, 0:SUB, 0:HID], nsum, ALU.add).then_inc(agg_read, 1)

            def wide(v, n):
                return v.rearrange("p (s a) -> p s a", a=1).to_broadcast([P, SUB, n])

            def neighbours(c):
                at = ds(c * SUB, SUB)
                nc.vector.scalar_tensor_tensor(out=den, in0=e0[:, at], scalar=float(N), in1=den,
                                               op0=ALU.mult, op1=ALU.add).then_inc(den_step, 1)
                dve.wait_ge(den_step, 4 * c + 2)
                nc.vector.reciprocal(den, den).then_inc(den_step, 1)
                dve.wait_ge(den_step, 4 * c + 3)
                nc.vector.tensor_tensor(aw, e1[:, at], den, ALU.mult)
                nc.vector.tensor_tensor(ew, e0[:, at], den, ALU.mult).then_inc(den_step, 1)
                dve.wait_ge(den_step, 4 * c + 4)
                dve.wait_ge(agg_read, c + 1 + 1)
                nc.vector.tensor_tensor(nsum, nsum, wide(aw, HID), ALU.mult)
                nc.vector.tensor_tensor(wc, csum.rearrange("p (a d) -> p a d", a=1).to_broadcast([P, SUB, HID]),
                                        wide(ew, HID), ALU.mult).then_inc(wc_made, 1)
                dve.wait_ge(wc_made, c + 1)
                nc.vector.tensor_tensor(nsum, nsum, wc, ALU.add).then_inc(nb_made, 1)

            def finish(c):
                dve.wait_ge(y_done, c + 1 + 1)
                dve.wait_ge(out_stored, 16 * c + 16)
                nc.vector.tensor_tensor(y, ps[:, 5, :].rearrange("p (s d) -> p s d", s=SUB),
                                        x2_sb[:, ds(c * SUB, SUB), :], ALU.add)\
                    .then_inc(y_step, 1)
                dve.wait_ge(y_step, 3 * c + 1 + 1)
                for s in range(SUB):
                    last = nc.vector.bn_stats(ybn[:, s, :], y[:, s, :])
                last.then_inc(y_step, 1)
                dve.wait_ge(y_step, 3 * c + 2 + 1)
                settle(dve)
                for s in range(SUB):
                    last = nc.vector.bn_aggr(ymv[:, s, :], ybn[:, s, :])
                last.then_inc(y_step, 1)
                dve.wait_ge(yr_step, 2 * c + 2)
                for s in range(SUB):
                    last = nc.vector.tensor_scalar(y[:, s, :], y[:, s, :], ymv[:, s, 0:1], yrs[:, s:s + 1],
                                                   ALU.subtract, ALU.mult)
                last.then_inc(y_normed, 1)
                dve.wait_ge(y_normed, 2 * c + 1)
                nc.vector.tensor_tensor(y, y, gamma_r.rearrange("p (a d) -> p a d", a=1)
                                        .to_broadcast([P, SUB, D]), ALU.mult).then_inc(y_normed, 1)
                dve.wait_ge(y_normed, 2 * c + 2)
                nc.vector.tensor_tensor(y, y, beta_r.rearrange("p (a d) -> p a d", a=1)
                                        .to_broadcast([P, SUB, D]), ALU.add).then_inc(out_made, 1)

            edge_blocks(0, range(NK))
            read_agg(0)
            with dve.Fori(1, NC) as c:
                edge_blocks(c, range(0, 1))
                neighbours(c - 1)
                edge_blocks(c, range(1, NK))
                finish(c - 1)
                read_agg(c)
            neighbours(NC - 1)
            finish(NC - 1)

        wc_made = sem("wc_made")

        def layer2_tensor(pe):
            pe.sem_inc(edges_used, ES)
            pe.sem_inc(y_done, 1)
            pe.sem_inc(nb_turned, 1)
            for t in range(NT):
                last = nc.tensor.matmul(ps[:, 5, 0:AGG], ones_b[:, :], h3[:, t, 0:AGG], start=t == 0, stop=t == NT - 1)
            last.then_inc(ones_done, 1)

            def aggregate(c, kbs):
                for kb in kbs:
                    pe.wait_ge(edges_made, c * NK + kb + 1)
                    if kb == 0:
                        pe.wait_ge(agg_read, c + 1)
                    for k in range(KB):
                        for s in range(SUB):
                            last = nc.tensor.matmul(ps[:, s, 0:AGG], edges[kb % 2 if NK > 1 else 0][:, k, s * P:(s + 1) * P],
                                                    h3[:, kb * KB + k, 0:AGG], start=kb == 0 and k == 0,
                                                    stop=kb == NK - 1 and k == KB - 1)
                    last.then_inc(edges_used, 1)

            def post(c):
                pe.wait_ge(nb_made, c + 1 + 1)
                settle(pe)
                for s in range(SUB):
                    last = nc.tensor.transpose(ps[0:HID, 4, s * P:(s + 1) * P], nsum[:, s, :], identf[:, :])
                last.then_inc(nb_turned, 1)
                pe.wait_ge(nbT_made, c + 1)
                pe.wait_ge(y_step, 3 * c + 1)
                for s in range(SUB):
                    last = nc.tensor.matmul(ps[:, 5, s * D:(s + 1) * D], nbT[0:HID, s * P:(s + 1) * P],
                                            wpT[0:HID, :], start=True, stop=True)
                last.then_inc(y_done, 1)

            aggregate(0, range(NK))
            with pe.Fori(1, NC) as c:
                aggregate(c, range(0, 1))
                post(c - 1)
                aggregate(c, range(1, NK))
            post(NC - 1)

        block = ctx.enter_context(nc.Block())

        gm_words = mask_t[:, NT * CH:2 * NT * CH].bitcast(F32)
        gm_adj = gm_words[:, 0:N].bitcast(I32)
        gm_mask = gm_words[:, N:N + N // 2].bitcast(BF16)
        gm_q = q_pack[:, 0, :, :].rearrange("p h q -> p (h q)")[:, 0:H * P].rearrange("p (h q) -> p h q", h=H)
        gm_s = pool_words[:, 0:N]
        gm_c = pool_words[:, N:N + 2 * H].rearrange("p (a h) -> p a h", h=H)
        gm_c3 = pool_words[:, N + 2 * H:N + 4 * H].bitcast(BF16)[:, 0:3 * H].rearrange("p (a h) -> p a h", h=H)
        gm_ct = pool_words[:, N + 4 * H:N + 4 * H + P // 2].bitcast(BF16)
        gm_loaded = sem("gm_loaded")
        gm_converted = sem("gm_converted")
        gm_scored = sem("gm_scored")
        gm_masked = sem("gm_masked")
        gm_maxed = sem("gm_maxed")
        gm_split = sem("gm_split")
        gm_turned = sem("gm_turned")
        gm_copied = sem("gm_copied")
        gm_stored = sem("gm_stored")
        gm_phase = sem("gm_phase")

        def exact_maximum(eng, program):
            eng.wait_ge(flag_made, 3)
            too_large = eng.value_load(flag[0:1, 0:1], min_val=0, max_val=1)
            with eng.If(too_large > 0):
                program(eng)
                eng.drain().then_inc(gm_phase, 1)
                eng.wait_ge(gm_phase, 5)
                settle(eng)

        def maximum_sync(sp):
            sp.sem_inc(gm_stored, 16)
            with sp.Fori(0, NT) as T:
                sp.wait_ge(gm_stored, 16 * T + 16)
                sp.dma_start(gm_adj, adj[ds(T * P, P), :]).then_inc(gm_loaded, 16)
                sp.dma_start(gm_q[0:KW, :, :], q_dram[T, :, :, :]).then_inc(gm_loaded, 16)
                sp.wait_ge(gm_copied, T + 1)
                sp.dma_start(q_dram[T, PARTS:KW, :, :].rearrange("k h q -> (k h) q"), gm_ct[0:3 * H, :])\
                    .then_inc(gm_stored, 16)
            sp.wait_ge(gm_stored, 16 * NT + 16)

        def maximum_none(eng):
            eng.sem_inc(settled, 1)

        def maximum_vector(dve):
            dve.sem_inc(gm_maxed, 1)
            with dve.Fori(0, NT) as T:
                dve.wait_ge(gm_loaded, 32 * T + 32)
                nc.vector.tensor_scalar(gm_mask, gm_adj, 0.0, -HUGE, ALU.is_equal, ALU.mult)\
                    .then_inc(gm_converted, 1)
                dve.wait_ge(gm_converted, T + 1)
                settle(dve)
                with dve.Fori(0, H) as h:
                    n = T * H + h
                    dve.wait_ge(gm_scored, n + 1)
                    dve.wait_ge(gm_maxed, n + 1)
                    nc.vector.tensor_tensor(gm_s, ps[:, 0:NC, :].rearrange("p b n -> p (b n)"), gm_mask,
                                            ALU.add).then_inc(gm_masked, 1)
                    dve.wait_ge(gm_masked, n + 1)
                    nc.vector.tensor_reduce(gm_c[:, 0, ds(h, 1)], gm_s, AX.X, ALU.max, negate=True)\
                        .then_inc(gm_maxed, 1)
                dve.wait_ge(gm_maxed, T * H + H + 1)
                settle(dve)
                nc.vector.tensor_copy(gm_c3[:, 0, :], gm_c[:, 0, :]).then_inc(gm_split, 1)
                dve.wait_ge(gm_split, 4 * T + 1)
                nc.vector.tensor_tensor(gm_c[:, 1, :], gm_c[:, 0, :], gm_c3[:, 0, :], ALU.subtract)\
                    .then_inc(gm_split, 1)
                dve.wait_ge(gm_split, 4 * T + 2)
                nc.vector.tensor_copy(gm_c3[:, 1, :], gm_c[:, 1, :]).then_inc(gm_split, 1)
                dve.wait_ge(gm_split, 4 * T + 3)
                nc.vector.tensor_tensor(gm_c3[:, 2, :], gm_c[:, 1, :], gm_c3[:, 1, :], ALU.subtract)\
                    .then_inc(gm_split, 1)
                dve.wait_ge(gm_turned, T + 1)
                nc.vector.tensor_copy(gm_ct[0:3 * H, :], bank16[0][0:3 * H, 0:P]).then_inc(gm_copied, 1)

        def maximum_tensor(pe):
            with pe.Fori(0, NT) as T:
                pe.wait_ge(gm_loaded, 32 * T + 32)
                settle(pe)
                with pe.Fori(0, H) as h:
                    pe.wait_ge(gm_maxed, T * H + h + 1)
                    for kb in range(NC):
                        last = nc.tensor.matmul(ps[:, kb, :], gm_q[0:KW, h, :],
                                                k_view[0:KW, h, kb * CH:(kb + 1) * CH], start=True, stop=True)
                    last.then_inc(gm_scored, 1)
                pe.wait_ge(gm_split, 4 * T + 4)
                settle(pe)
                nc.tensor.transpose(bank16[0][0:3 * H, 0:P], gm_c3.rearrange("p a h -> p (a h)"), ident[:, :])\
                    .then_inc(gm_turned, 1)

        def settle(eng):
            eng.sem_inc(settled, 1)

        def phase_end(eng, n):
            eng.drain().then_inc(phase, 1)
            eng.wait_ge(phase, 5 * n)

        @block.sync
        def _(sp):
            def load_adj(X):
                sp.wait_ge(converted, X + ONE)
                sp.wait_ge(mask_stored, 16 * X + 16)
                c, i = (X % (NC * MB)) // MB, X % MB
                src = adj[ds(c * CH, CH), ds(i * 2 * P, 2 * P)].rearrange("(s p) k -> p s k", p=P)
                sp.dma_start(adj_in[:, :, :], src).then_inc(adj_loaded, 16)

            def store_mask(X, c, i, slot):
                sp.wait_ge(evacuated, 2 * X + 2 + TP)
                src = m_view[:, slot, ds(2 * i, 2), :]
                sp.dma_start(m_dram[c, :, ds(2 * i, 2), :], src).then_inc(mask_stored, 16)

            def store_q(T, u):
                sp.wait_ge(q_out_made, T + 1 + ONE)
                sp.dma_start(q_dram[T, :, :, :], q_out[0:KW, u, :, :]).then_inc(q_stored[u], 16)

            def store_v(T, u):
                sp.wait_ge(hi_made, T + 1 + 2)
                sp.dma_start(v_dram[:, T, :, :].rearrange("g p k -> p g k"),
                             v_out[:, u, :, :].rearrange("p (g h) k -> p g (h k)", g=2))\
                    .then_inc(v_stored[u], 16)

            sp.sem_inc(mask_stored, 32)
            for u in range(RING):
                sp.sem_inc(q_stored[u], 16)
                sp.sem_inc(v_stored[u], 16)
            for g in range(2):
                sp.sem_inc(acc_stored[g], 16)
            xv = x.rearrange("(t p) d -> p t d", p=P)
            for j in range(4):
                w = NT // 4
                sp.dma_start(x_sb[:, j * w:(j + 1) * w, :], xv[:, j * w:(j + 1) * w, :]).then_inc(x_in[j], 16)
            sp.dma_start(wqkv, w_qkv).then_inc(params_in, 16)
            for k, v in enumerate((g1, be1)):
                sp.dma_start(cols[:, k:k + 1], v.rearrange("(p a) -> p a", a=1)).then_inc(params_in, 16)

            load_adj(0)
            for u in range(2):
                store_v(u, u)

            def steps_of(i, last):
                for u in range(RING):
                    T, X = RING * i + u, 2 * i + u // 2
                    if u % 2 == 0:
                        load_adj(X + 1)
                    if not (last and u + 2 >= RING):
                        store_v(T + 2, (u + 2) % RING)
                    store_q(T, u)
                    if u % 2:
                        store_mask(X, 0, X, 0)
            with sp.Fori(0, NT // RING - 1) as i:
                steps_of(i, False)
            steps_of(NT // RING - 1, True)
            for u in range(RING):
                sp.wait_ge(q_stored[u], 16 * (NT // RING + 1))
                sp.wait_ge(v_stored[u], 16 * (NT // RING + 1))
            phase_end(sp, 1)
            exact_maximum(sp, maximum_sync)

            def load_q(c, g):
                for hh in range(HG):
                    src = q_dram[ds(c * SUB, SUB), :, g * HG + hh, :].rearrange("s k q -> k s q")
                    sp.dma_start(q_pack[0:KW, g, hh, :].rearrange("k (s q) -> k s q", q=P), src)\
                        .then_inc(q_loaded[g], 16)

            def load_v(BI, h):
                sp.wait_ge(pv_done, 4 * BI + 2 * h + 2)
                b, g = BI % NB, (BI // NB) % 2
                src = v_dram[g, ds(b * SLOTS + 2 * h, 2), :, :]
                sp.dma_start(v_st[:, 2 * h:2 * h + 2, :], src.rearrange("t p k -> p t k"))\
                    .then_inc(v_loaded[h], 16)

            def body(c, g, b, prep):
                BI = (c * 2 + g) * NB + b
                i = b + g * NB
                X = (c + 1) * MB + i
                if prep:
                    load_adj(X + 1)
                load_v(BI + 1, 0)
                if prep:
                    store_mask(X, c + 1, i, (c + 1) % 2)
                load_v(BI + 1, 1)

            def store_acc(c, g):
                sp.wait_ge(acc_copied[g], c + 1 + ONE)
                sp.dma_start(a_dram[c, :, g, :], acc_sb[:, g, :]).then_inc(acc_stored[g], 16)

            def segment(c, g, prep, before):
                if NB > 1:
                    with sp.Fori(0, NB - 1) as b:
                        body(c, g, b, prep)
                body(c, g, NB - 1, prep)
                if before is not None:
                    store_acc(*before)

            load_q(0, 0)
            for h in range(2):
                load_v(0, h)
            load_q(0, 1)

            def chunk(c, prep, first):
                segment(c, 0, prep, None if first else (c - 1, 1))
                if prep:
                    sp.wait_ge(scored, (2 * c + 1) * SEG_UNITS)
                    load_q(c + 1, 0)
                segment(c, 1, prep, (c, 0))
                if prep:
                    sp.wait_ge(scored, (2 * c + 2) * SEG_UNITS)
                    load_q(c + 1, 1)

            chunk(0, True, True)
            if NC > 2:
                with sp.Fori(1, NC - 1) as c:
                    chunk(c, True, False)
            chunk(NC - 1, False, False)
            store_acc(NC - 1, 1)
            for g in range(2):
                sp.wait_ge(acc_stored[g], 16 * (NC + 1))
                sp.wait_ge(v_loaded[g], 16 * (2 * NC * NB + 1))
            sp.wait_ge(adj_loaded, 16 * (NC * MB + 1))
            sp.wait_ge(mask_stored, 16 * (NC * MB + 2))
            phase_end(sp, 2)
            tail_sync(sp)

        @block.gpsimd
        def _(pool):
            pool.sem_inc(sq_made, RING)
            nc.gpsimd.memset(ident[:, :], 0.0)
            nc.gpsimd.memset(ones_b[:, :], 1.0)
            nc.gpsimd.memset(identf[:, :], 0.0)
            nc.gpsimd.memset(zeros[:, :], 0.0)
            nc.gpsimd.memset(cols[:, 8:9], -0.5)
            nc.gpsimd.memset(cols[:, 9:10], EPS)
            nc.gpsimd.memset(v_out[:, :, :, HD:VW], 1.0)
            nc.gpsimd.memset(packed[:, :, 0:H, PARTS:KW], 0.0)
            nc.gpsimd.memset(packed[:, :, H:2 * H, PARTS:KW], 1.0).then_inc(ident_zeroed, 1)
            pool.wait_ge(ident_zeroed, 1)
            for m in (ident, identf):
                last = nc.gpsimd.affine_select(out=m[:, :], in_=m[:, :], compare_op=ALU.not_equal, fill=1.0,
                                               base=0, pattern=[[-1, P]], channel_multiplier=1)
            last.then_inc(const_made, 1)
            pool.wait_ge(const_made, 1)
            w = NT // 4
            for j in range(4):
                at = slice(j * w, j * w + w)
                pool.wait_ge(var_made, j + 1)
                nc.gpsimd.tensor_scalar(rstd[:, at], mv[:, at, 1], EPS, None, ALU.add).then_inc(eps_added, 1)
                pool.wait_ge(eps_added, j + 1)
                nc.gpsimd.tensor_tensor(rstd[:, at], rstd[:, at], cols[:, 8:9].to_broadcast([P, w]), ALU.pow)\
                    .then_inc(rstd_made, 1)

            def stage1(T, u):
                pool.wait_ge(norms_made, T + 1)
                pool.wait_ge(hi_made, T + 1 + 2)
                nc.gpsimd.tensor_tensor(sq[:, u % 2, :].rearrange("p (h k) -> p h k", k=HD),
                                        packed[:, u, :, 0:HD], packed[:, u, :, 0:HD], ALU.mult)\
                    .then_inc(sq_made, 1)

            with pool.Fori(0, NT // RING) as i:
                for u in range(RING):
                    stage1(RING * i + u, u)
            phase_end(pool, 1)
            pool.wait_ge(bound_step, 1)
            nc.gpsimd.partition_all_reduce(small[:, 1, :], small[:, 0, :], P, bass.bass_isa.ReduceOp.max)\
                .then_inc(bound_step, 1)
            exact_maximum(pool, maximum_none)
            phase_end(pool, 2)
            tail_gpsimd(pool)

        @block.scalar
        def _(act):
            act.sem_inc(hT_made, 2)
            act.sem_inc(hi_made, 2)
            act.sem_inc(q_out_made, ONE)
            act.wait_ge(params_in, 48)

            def norm_turned(T, u):
                act.wait_ge(xT_done, T + 1 + XN)
                act.wait_ge(qkv_done, T + 1)
                nc.scalar.activation(hT[:, u, :], ps[:, u % 2, 0:P], ACT.Identity, bias=cols[:, 1:2],
                                     scale=cols[:, 0:1]).then_inc(hT_made, 1)

            def split(i, T, u):
                q = ps[:, 2 + u % 2, 0:D].rearrange("p (h a k) -> p h a k", h=H, a=1)
                k = ps[:, 2 + u % 2, D:2 * D].rearrange("p (h a k) -> p h a k", h=H, a=1)
                act.wait_ge(qkv_done, T + 1 + RING)
                act.wait_ge(nT_done, T + 1)
                act.wait_ge(sq_made, T + 1)
                act.wait_ge(v_stored[u], 16 * i + 16)
                nc.scalar.activation(packed[:, u, 0:H, 0:48].rearrange("p h (a k) -> p h a k", a=3),
                                     q.to_broadcast([P, H, 3, HD]), ACT.Copy)
                nc.scalar.activation(packed[:, u, H:, 64:96].rearrange("p h (a k) -> p h a k", a=2),
                                     k.to_broadcast([P, H, 2, HD]), ACT.Copy)
                nc.scalar.activation(packed[:, u, H:, 0:HD], k[:, :, 0, :], ACT.Copy)
                nc.scalar.activation(v_out[:, u, :, 0:HD],
                                     ps[:, 2 + u % 2, 2 * D:3 * D].rearrange("p (h k) -> p h k", h=H),
                                     ACT.Copy).then_inc(hi_made, 1)

            def evac_q(i, T, u):
                act.wait_ge(nT_done, T + 1 + RING)
                act.wait_ge(q_stored[u], 16 * i + 16)
                nc.scalar.activation(q_out[0:KW, u, :, :].rearrange("p h q -> p (h q)"),
                                     bank16[4][0:KW, :], ACT.Copy).then_inc(q_out_made, 1)

            for u in range(3):
                norm_turned(u, u)
            for u in range(2):
                split(0, u, u)

            def steps_of(i, last):
                for u in range(RING):
                    T = RING * i + u
                    if not (last and u + 3 >= RING):
                        norm_turned(T + 3, (u + 3) % RING)
                    if not (last and u + 2 >= RING):
                        split(i + (u + 2) // RING, T + 2, (u + 2) % RING)
                    evac_q(i, T, u)
            with act.Fori(0, NT // RING - 1) as i:
                steps_of(i, False)
            steps_of(NT // RING - 1, True)
            phase_end(act, 1)
            exact_maximum(act, maximum_none)

            act.sem_inc(exped, SB2)

            with act.Fori(0, 2 * NC * NB) as BI:
                for k in range(SLOTS):
                    TL = BI * SLOTS + k
                    act.wait_ge(pv_done, TL + 1)
                    for pair in range(2):
                        act.wait_ge(scored, 2 * TL + pair + 1)
                        nc.scalar.activation(probs[:, k, pair, :],
                                             ps[:, 2 * pair:2 * pair + 2, :].rearrange("p a q -> p (a q)"),
                                             ACT.Exp).then_inc(exped, 1)
            phase_end(act, 2)
            tail_scalar(act)

        @block.vector
        def _(dve):
            dve.sem_inc(converted, ONE)
            dve.sem_inc(evacuated, TP)
            dve.sem_inc(r1_made, 2)
            dve.sem_inc(norms_made, 2)
            dve.sem_inc(k_made, 1)
            for g in range(2):
                dve.sem_inc(acc_copied[g], ONE)

            def convert(X):
                dve.wait_ge(adj_loaded, 16 * X + 16)
                dve.wait_ge(turned, 2 * X + TP)
                nc.vector.tensor_scalar(mask_n[:, :, :], adj_in[:, :, :], 0.0, -HUGE, ALU.is_equal, ALU.mult)\
                    .then_inc(converted, 1)

            def evac(X, slot, i, t):
                dve.wait_ge(turned, 2 * X + t + 1 + TP)
                nc.vector.tensor_copy(m_view[:, slot, 2 * i + t, :], bank16[6 + t][:, 0:CH]).then_inc(evacuated, 1)

            w = NT // 4
            for j in range(4):
                dve.wait_ge(x_in[j], 16)
                for t in range(j * w, j * w + w):
                    last = nc.vector.bn_stats(bn[:, t, :], x_sb[:, t, :])
                last.then_inc(bn_made, 1)
                dve.wait_ge(bn_made, j + 1)
                for t in range(j * w, j * w + w):
                    last = nc.vector.bn_aggr(mv[:, t, :], bn[:, t, :])
                last.then_inc(var_made, 1)
            dve.wait_ge(params_in, 48)
            nc.vector.tensor_scalar(wqkv[:, 0:D], wqkv[:, 0:D], SCALE, None, ALU.mult).then_inc(w_scaled, 1)
            dve.wait_ge(rstd_made, 4)

            def normalise(T, u):
                dve.wait_ge(xT_done, T + 1)
                nc.vector.tensor_scalar(xn[:, u % 2, :], x_sb[:, T, :], mv[:, T, 0:1], rstd[:, ds(T, 1)],
                                        ALU.subtract, ALU.mult).then_inc(xn_made, 1)

            def split(T, u):
                dve.wait_ge(hi_made, T + 1 + 2)
                r = r1[:, u % 2, :].rearrange("p (h a k) -> p h a k", k=HD, a=1)
                rq, rk = r[:, 0:H, 0, :], r[:, H:, 0, :]
                nc.vector.tensor_tensor(r[:, :, 0, :], ps[:, 2 + u % 2, 0:2 * D].rearrange("p (h k) -> p h k", k=HD),
                                        packed[:, u, :, 0:HD], ALU.subtract).then_inc(r1_made, 1)
                dve.wait_ge(r1_made, T + 1 + 2)
                nc.vector.tensor_copy(packed[:, u, 0:H, 48:80].rearrange("p h (a k) -> p h a k", a=2),
                                      r[:, 0:H, :, :].to_broadcast([P, H, 2, HD]))
                nc.vector.tensor_copy(packed[:, u, H:, 16:80].rearrange("p h (a k) -> p h a k", a=2)[:, :, :, 0:HD],
                                      r[:, H:, :, :].to_broadcast([P, H, 2, HD])).then_inc(mid_made, 1)
                dve.wait_ge(mid_made, T + 1)
                nc.vector.tensor_tensor(packed[:, u, 0:H, 80:96], rq, packed[:, u, 0:H, 64:80], ALU.subtract)
                nc.vector.tensor_tensor(packed[:, u, H:, 32:48], rk, packed[:, u, H:, 16:32], ALU.subtract)\
                    .then_inc(lo_made, 1)

            def sum_norms(T, u):
                dve.wait_ge(sq_made, T + 1 + RING)
                nc.vector.tensor_reduce(norms[:, T, :], sq[:, u % 2, :].rearrange("p (h k) -> p h k", k=HD),
                                        AX.X, ALU.add).then_inc(norms_made, 1)

            def evac_k(T):
                dve.wait_ge(nT_done, T + 1 + RING)
                nc.vector.tensor_copy(k_view[0:KW, :, ds(T * P, P)],
                                      bank16[5][0:KW, :].rearrange("p (h n) -> p h n", h=H)).then_inc(k_made, 1)

            for u in range(4):
                normalise(u, u)
            for u in range(2):
                split(u, u)
                sum_norms(u, u)

            def steps_of(i, last):
                for u in range(RING):
                    T, X = RING * i + u, 2 * i + u // 2
                    if not last:
                        normalise(T + 4, u)
                    if u % 2 == 0:
                        convert(X)
                    if not (last and u + 2 >= RING):
                        split(T + 2, (u + 2) % RING)
                    evac_k(T)
                    evac(X, 0, X, u % 2)
                    if not (last and u + 2 >= RING):
                        sum_norms(T + 2, (u + 2) % RING)
            with dve.Fori(0, NT // RING - 1) as i:
                steps_of(i, False)
            steps_of(NT // RING - 1, True)
            phase_end(dve, 1)
            nc.vector.tensor_reduce(small[:, 0, :], norms.rearrange("p t k -> p k t"), AX.X, ALU.max)\
                .then_inc(bound_step, 1)
            dve.wait_ge(bound_step, 2)
            nc.vector.tensor_tensor(small[:, 2, 0:H], small[:, 1, 0:H], small[:, 1, H:], ALU.mult)\
                .then_inc(flag_made, 1)
            dve.wait_ge(flag_made, 1)
            nc.vector.tensor_reduce(small[:, 3, 0:1], small[:, 2, 0:H], AX.X, ALU.max).then_inc(flag_made, 1)
            dve.wait_ge(flag_made, 2)
            nc.vector.tensor_scalar(flag[:, 0:1], small[:, 3, 0:1], SAFE * SAFE, None, ALU.is_gt)\
                .then_inc(flag_made, 1)
            exact_maximum(dve, maximum_vector)

            def mask(BI, c, b, k, pair, n):
                dve.wait_ge(exped, 2 * (BI * SLOTS + k) + pair + 1 + SB2)
                m = m_view[:, c % 2, b * SLOTS + k, :].rearrange("p (a q) -> p a q", a=1)
                pr = probs[:, k, pair, :].rearrange("p (a q) -> p a q", a=2)
                nc.vector.scalar_tensor_tensor(out=pr, in0=m.to_broadcast([P, 2, CH]), scalar=HUGE, in1=pr,
                                               op0=ALU.add, op1=ALU.min).then_inc(masked, 1)

            def body(c, g, b, prep):
                BI = (c * 2 + g) * NB + b
                i = b + g * NB
                X = (c + 1) * MB + i
                n = 0
                for k in range(SLOTS):
                    if prep and k == 1:
                        convert(X)
                    for pair in range(2):
                        if not (k % 2 and pair):
                            mask(BI, c, b, k, pair, n)
                            n += 1
                if prep:
                    for t in range(2):
                        evac(X, (c + 1) % 2, i, t)

            def copy_acc(c, g):
                dve.wait_ge(pv_done, ((2 * c + g) + 1) * NT + SLOTS)
                dve.wait_ge(acc_stored[g], 16 * c + 16)
                nc.vector.tensor_copy(acc_sb[:, g, :], ps[:, 4 + g, :]).then_inc(acc_copied[g], 1)

            def segment(c, g, prep, before):
                if NB > 1:
                    with dve.Fori(0, NB - 1) as b:
                        body(c, g, b, prep)
                body(c, g, NB - 1, prep)
                if before is not None:
                    copy_acc(*before)

            def chunk(c, prep, first):
                dve.wait_ge(evacuated, (c + 1) * 2 * MB + TP)
                settle(dve)
                segment(c, 0, prep, None if first else (c - 1, 1))
                segment(c, 1, prep, (c, 0))

            chunk(0, True, True)
            if NC > 2:
                with dve.Fori(1, NC - 1) as c:
                    chunk(c, True, False)
            chunk(NC - 1, False, False)
            copy_acc(NC - 1, 1)
            phase_end(dve, 2)
            tail_vector(dve)

        @block.tensor
        def _(pe):
            pe.sem_inc(xT_done, XN)
            pe.sem_inc(qkv_done, RING)
            pe.sem_inc(nT_done, RING)
            pe.sem_inc(turned, TP)
            pe.sem_inc(pv_done, SLOTS)
            pe.wait_ge(const_made, 1)
            pe.wait_ge(w_scaled, 1)

            def turn_mask(X, t):
                pe.wait_ge(converted, X + 1 + ONE)
                pe.wait_ge(evacuated, 2 * X + t + 1)
                for s in range(SUB):
                    last = nc.tensor.transpose(bank16[6 + t][:, s * P:(s + 1) * P],
                                               mask_n[:, s, t * P:(t + 1) * P], ident[:, :])
                last.then_inc(turned, 1)

            def turn_x(T, u):
                pe.wait_ge(xn_made, T + 1)
                pe.wait_ge(hT_made, T + 1)
                nc.tensor.transpose(ps[:, u % 2, 0:P], xn[:, u % 2, :], identf[:, :]).then_inc(xT_done, 1)

            def qkv(T, u):
                pe.wait_ge(hT_made, T + 1 + 2)
                pe.wait_ge(hi_made, T + 1)
                pe.wait_ge(r1_made, T + 1)
                nc.tensor.matmul(ps[:, 2 + u % 2, 0:3 * D], hT[:, u, :], wqkv, start=True, stop=True)\
                    .then_inc(qkv_done, 1)

            def turn_packed(T, u):
                pe.wait_ge(lo_made, T + 1)
                pe.wait_ge(k_made, T + 1)
                pe.wait_ge(q_out_made, T + 1)
                for h in range(2 * H):
                    b, j = 4 + h // H, h % H
                    last = nc.tensor.transpose(bank16[b][0:KW, j * P:(j + 1) * P], packed[:, u, h, 0:KW],
                                               ident[:, :])
                last.then_inc(nT_done, 1)

            for u in range(3):
                turn_x(u, u)
            for u in range(2):
                qkv(u, u)

            def steps_of(i, last):
                for u in range(RING):
                    T, X = RING * i + u, 2 * i + u // 2
                    if not (last and u + 3 >= RING):
                        turn_x(T + 3, (u + 3) % RING)
                    if not (last and u + 2 >= RING):
                        qkv(T + 2, (u + 2) % RING)
                    turn_packed(T, u)
                    turn_mask(X, u % 2)
            with pe.Fori(0, NT // RING - 1) as i:
                steps_of(i, False)
            steps_of(NT // RING - 1, True)
            phase_end(pe, 1)
            exact_maximum(pe, maximum_tensor)

            def scores(c, g, b, k, fresh, shifted):
                TL = ((c * 2 + g) * NB + b) * SLOTS + k
                if fresh:
                    pe.wait_ge(q_loaded[g], 64 * c + 64)
                for pair in range(2):
                    by_pe = shifted or (k % 2 and pair)
                    if by_pe:
                        pe.wait_ge(evacuated, c * NT + b * SLOTS + k + 1 + TP)
                    pe.wait_ge(exped, 2 * TL + pair + 1)
                    for j in range(2):
                        hh = 2 * pair + j
                        bank = ps[:, 2 * pair + j, :]
                        kt = k_view[0:KW, g * HG + hh, ds((b * SLOTS + k) * P, P)]
                        last = nc.tensor.matmul(bank, kt, q_pack[0:KW, g, hh, :], start=True, stop=not by_pe)
                        if by_pe:
                            last = nc.tensor.matmul(bank, ident[:, :], m_view[:, c % 2, b * SLOTS + k, :],
                                                    start=False, stop=True)
                    last.then_inc(scored, 1)

            def products(c, g, b, k):
                BI = (c * 2 + g) * NB + b
                if k % 2 == 0:
                    pe.wait_ge(v_loaded[k // 2], 16 * BI + 16)
                pe.wait_ge(masked, 6 * BI + (2, 3, 5, 6)[k])
                if k % 2:
                    pe.wait_ge(exped, 2 * (BI * SLOTS + k) + 2 + SB2)
                for hh in range(HG):
                    last = nc.tensor.matmul(ps[32 * hh:32 * hh + VW, 4 + g, :],
                                            v_st[:, k, hh * VW:(hh + 1) * VW],
                                            probs[:, k, hh // 2, (hh % 2) * CH:(hh % 2 + 1) * CH],
                                            start=False, stop=False, skip_group_check=True)
                last.then_inc(pv_done, 1)

            def clear(c, g):
                pe.wait_ge(acc_copied[g], c + 1)
                nc.tensor.matmul(ps[:, 4 + g, :], zeros[:, 0:P], zeros[:, :], start=True, stop=True,
                                 skip_group_check=True)

            def body(c, g, b, nxt, prep, shifted):
                X = (c + 1) * MB + b + g * NB
                for k in range(SLOTS):
                    ahead = k + LEAD - SLOTS
                    if ahead < 0:
                        scores(c, g, b, k + LEAD, False, shifted)
                    elif nxt is not None:
                        cn, gn, bn_ = nxt
                        scores(cn, gn, bn_, ahead, isinstance(bn_, int) and ahead == 0, shifted)
                    products(c, g, b, k)
                    if prep and k == 1:
                        for t in range(2):
                            turn_mask(X, t)

            def segment(c, g, nxt, prep, shifted):
                clear(c, g)
                if NB > 1:
                    with pe.Fori(0, NB - 1) as b:
                        body(c, g, b, (c, g, b + 1), prep, shifted)
                body(c, g, NB - 1, nxt, prep, shifted)

            def attention(shifted):
                for k in range(LEAD):
                    scores(0, 0, 0, k, k == 0, shifted)
                with pe.Fori(0, NC - 1) as c:
                    segment(c, 0, (c, 1, 0), True, shifted)
                    segment(c, 1, (c + 1, 0, 0), True, shifted)
                segment(NC - 1, 0, (NC - 1, 1, 0), False, shifted)
                segment(NC - 1, 1, None, False, shifted)

            too_large = pe.value_load(flag[0:1, 0:1], min_val=0, max_val=1)
            with pe.If(too_large > 0):
                attention(True)
            with pe.Else():
                attention(False)
            phase_end(pe, 2)
            tail_tensor(pe)


_INS = ["x", "adj", "L0_gnn_w_qkv", "L0_gnn_w_proj", "L0_gnn_b_proj", "L0_gnn_w1", "L0_gnn_b1", "L0_gnn_w2",
        "L0_gnn_b2", "L0_gnn_g1", "L0_gnn_be1", "L0_gnn_g2", "L0_gnn_be2", "L1_gnn_Wt", "L1_gnn_bt",
        "L1_gnn_Wa", "L1_gnn_ba", "L1_gnn_Wp", "L1_gnn_bp", "L1_gnn_gamma", "L1_gnn_beta"]


def kernel(**inputs):
    import numpy as np
    import concourse.bacc as bacc
    from concourse.bass_utils import run_bass_kernel_spmd

    nc = bacc.Bacc("TRN2", target_bir_lowering=False, num_devices=1)
    arrays = {f"in_{name}": np.ascontiguousarray(inputs[name]) for name in _INS}
    args = [nc.dram_tensor(name, a.shape, mybir.dt.from_np(a.dtype), kind="ExternalInput").ap()
            for name, a in arrays.items()]
    out = nc.dram_tensor("out_0", arrays["in_x"].shape, F32, kind="ExternalOutput").ap()
    gnn_kernel(nc, *args, out)
    return run_bass_kernel_spmd(nc, [arrays], core_ids=[0]).results[0]["out_0"]
```

```python
from contextlib import ExitStack

import concourse.bass as bass
from concourse import mybir

F32 = mybir.dt.float32
BF16 = mybir.dt.bfloat16
I32 = mybir.dt.int32
ALU = mybir.AluOpType
ACT = mybir.ActivationFunctionType
AX = mybir.AxisListType
ds = bass.ds

P = 128
D = 128
H, HD = 8, 16
HG = H // 2
CH = 512
SUB = CH // P
PARTS = 6 * HD
KW = PARTS + 3
PACK = 100
VW = HD + 1
SLOTS = 4
RING = 4
LEAD = 3
FF = 512
HID = 64
HUGE = 2.0 ** 127
NEG = -9000000000000000.0
SAFE = 38.0
EPS = 1e-5


def gnn_kernel(nc, x, adj, w_qkv, w_proj, b_proj, w1, b1, w2, b2, g1, be1, g2, be2,
               Wt, bt, Wa, ba, Wp, bp, gamma, beta, out):
    N = x.shape[0]
    NT, NC = N // P, N // CH
    NB = NT // SLOTS
    MB = NT // 2
    SEG_UNITS = 2 * NT
    SCALE = float(HD) ** -0.5

    q_dram = nc.dram_tensor("q_packed", (NT, KW, H, P), BF16).ap()
    v_dram = nc.dram_tensor("v_ones", (2, NT, P, HG * VW), F32).ap()
    m_dram = nc.dram_tensor("mask_t", (NC, P, NT, CH), BF16).ap()
    a_dram = nc.dram_tensor("attn_t", (NC, P, 2, CH), F32).ap()

    with ExitStack() as ctx:
        def sb(name, shape, dt):
            return ctx.enter_context(nc.sbuf_tensor(name, shape, dt))

        def sem(name):
            return ctx.enter_context(nc.semaphore(name))

        k_pack = sb("k_pack", [P, max(H * N, 32768)], BF16)
        mask_t = sb("mask_t_sb", [P, max(2 * NT * CH, 32768)], BF16)
        q_pack = sb("q_pack", [P, 2, HG, CH], BF16)
        probs = sb("probs", [P, SLOTS, 2, 2 * CH], F32)
        v_st = sb("v_st", [P, SLOTS, HG * VW], F32)
        adj_in = sb("adj_in", [P, SUB, 2 * P], I32)
        mask_n = sb("mask_n", [P, SUB, 2 * P], BF16)
        acc_sb = sb("acc_sb", [P, 2, CH], F32)
        tail_words = sb("tail_words", [P, 4096], F32)
        ident = sb("ident", [P, P], BF16)
        identf = sb("identf", [P, P], F32)
        ones_b = sb("ones_b", [P, P], BF16)
        zeros = sb("zeros", [1, CH], BF16)
        cols = sb("cols", [P, 16], F32)
        small = sb("small", [P, 8, 16], F32)
        flag = sb("flag", [P, 2], I32)
        ps = ctx.enter_context(nc.psum_tensor("ps", [P, 8, CH], F32))

        m_view = mask_t[:, 0:2 * NT * CH].rearrange("p (s t q) -> p s t q", s=2, t=NT)
        k_view = k_pack[:, 0:H * N].rearrange("p (h n) -> p h n", h=H)
        bank16 = [ps[:, b, :].bitcast(BF16) for b in range(8)]

        x_sb = mask_t[:, NT * CH:].bitcast(F32)[:, 0:NT * D].rearrange("p (t d) -> p t d", d=D)
        stat_area = mask_t[:, NT * CH:].bitcast(F32)[:, NT * D:]
        taken = [0]

        def stat(n):
            taken[0] += n
            return stat_area[:, taken[0] - n:taken[0]]
        bn = stat(6 * NT).rearrange("p (t k) -> p t k", k=6)
        mv = stat(2 * NT).rearrange("p (t k) -> p t k", k=2)
        rstd = stat(NT)
        norms = stat(16 * NT).rearrange("p (t k) -> p t k", k=16)
        pool_words = probs[:, :, :, :].rearrange("p a b c -> p (a b c)")
        used = [0]

        def part(n):
            used[0] += n
            return pool_words[:, used[0] - n:used[0]]
        packed = part(RING * 16 * PACK // 2).bitcast(BF16).rearrange("p (u h k) -> p u h k", u=RING, h=16)
        r1 = part(512).rearrange("p (u n) -> p u n", u=2)
        sq = part(512).rearrange("p (u n) -> p u n", u=2)
        xn = part(256).rearrange("p (u n) -> p u n", u=2)
        hT = part(RING * P).rearrange("p (u n) -> p u n", u=RING)
        v_out = part(RING * H * VW).rearrange("p (u h k) -> p u h k", u=RING, h=H)
        q_out = part(RING * H * P // 2).bitcast(BF16).rearrange("p (u h q) -> p u h q", u=RING, h=H)
        wqkv = part(3 * D)

        phase = sem("phase")
        settled = sem("settled")
        params_in = sem("params_in")
        x_in = [sem(f"x_in{j}") for j in range(4)]
        w_scaled = sem("w_scaled")
        const_made = sem("const_made")
        ident_zeroed = sem("ident_zeroed")
        bn_made = sem("bn_made")
        var_made = sem("var_made")
        eps_added = sem("eps_added")
        rstd_made = sem("rstd_made")
        xn_made = sem("xn_made")
        xT_done = sem("xT_done")
        hT_made = sem("hT_made")
        qkv_done = sem("qkv_done")
        hi_made = sem("hi_made")
        r1_made = sem("r1_made")
        mid_made = sem("mid_made")
        lo_made = sem("lo_made")
        sq_made = sem("sq_made")
        norms_made = sem("norms_made")
        nT_done = sem("nT_done")
        q_out_made = sem("q_out_made")
        k_made = sem("k_made")
        q_stored = [sem(f"q_stored{u}") for u in range(RING)]
        v_stored = [sem(f"v_stored{u}") for u in range(RING)]
        bound_step = sem("bound_step")
        flag_made = sem("flag_made")
        adj_loaded = sem("adj_loaded")
        converted = sem("converted")
        turned = sem("turned")
        evacuated = sem("evacuated")
        mask_stored = sem("mask_stored")
        q_loaded = [sem("q_loaded0"), sem("q_loaded1")]
        v_loaded = [sem("v_loaded0"), sem("v_loaded1")]
        scored = sem("scored")
        exped = sem("exped")
        masked = sem("masked")
        pv_done = sem("pv_done")
        acc_copied = [sem("acc_copied0"), sem("acc_copied1")]
        acc_stored = [sem("acc_stored0"), sem("acc_stored1")]

        XN, TP, SB2, ONE = 2, 2, 2, 1

        w_words = k_pack[:, :].bitcast(F32)

        def taker(words):
            at = [0]

            def take(*shape):
                n = 1
                for s in shape:
                    n *= s
                at[0] += n
                assert at[0] <= words.shape[1]
                v = words[:, at[0] - n:at[0]]
                return v.rearrange("p (a b) -> p a b", b=shape[-1]) if len(shape) > 1 else v
            return take
        wb, pb, lb = taker(w_words), taker(pool_words), taker(tail_words)

        x2_sb = wb(NT, D)
        h3 = wb(NT * 98).bitcast(BF16).rearrange("p (t k) -> p t k", k=196)
        s_row = wb(NT)
        w1_sb, w2_sb, wp_sb = lb(FF), lb(FF // P, D), lb(D)
        wtT, wpT = wb(HID), wb(D)
        wt_raw, wpr_raw = lb(D), lb(HID)
        bproj_r, b2_r, bp_r, gamma_r, beta_r = lb(D), lb(D), lb(D), lb(D), lb(D)
        bt_r, wa_r, ba_r, csum = lb(HID), lb(HID), lb(1), wb(HID)
        b1_c, g2_c, be2_c = lb(FF // P), lb(1), lb(1)
        e1, e0, mx = wb(NT), wb(NT), wb(NT)

        acc, xr, xb = lb(2, CH), lb(SUB, D), pb(SUB, D)
        att, attT, x1 = pb(SUB * H, HD), pb(CH), pb(SUB, D)
        h2, h2T, x2 = pb(SUB, D), pb(CH), pb(SUB, D)
        ff = pb(FF // P, CH)
        x1b, x2T, hid, rest_h = wb(SUB, D), wb(CH), wb(SUB, HID), wb(SUB, HID)
        bn2, mv2, rl, rstd2 = wb(SUB, 6), wb(SUB, 2), wb(2 * SUB * HG), wb(SUB)
        B_FF, B_ACC, B_TURN, B_PROJ, B_OUT, B_X2, B_HID = 0, 4, 6, 7, 3, 4, 5

        tail_in = sem("tail_in")
        wT_turned, wT_copied = sem("wT_turned"), sem("wT_copied")
        acc_in = sem("acc_in")
        acc_turned = sem("acc_turned")
        rl_made, att_made = sem("rl_made"), sem("att_made")
        att_turned, attT_made = sem("att_turned"), sem("attT_made")
        projected = sem("projected")
        xb_made = sem("xb_made")
        x1_made, bn2_made, mv2_made = sem("x1_made"), sem("bn2_made"), sem("mv2_made")
        eps2_added, rstd2_made, x1b_made = sem("eps2_added"), sem("rstd2_made"), sem("x1b_made")
        h2_made, h2_turned, h2T_made = sem("h2_made"), sem("h2_turned"), sem("h2T_made")
        ff1_done, gelu_made, ff2_done = sem("ff1_done"), sem("gelu_made"), sem("ff2_done")
        x2_made, x2b_made, x2_turned, x2T_made = sem("x2_made"), sem("x2b_made"), sem("x2_turned"), sem("x2T_made")
        hid_done, hid_made, hid_step = sem("hid_done"), sem("hid_made"), sem("hid_step")
        NM = FF // P

        def per_row(v, n=D):
            return v.rearrange("p (a d) -> p a d", a=1).to_broadcast([P, SUB, n])

        def by_tile(bank, n=D):
            return ps[:, bank, 0:SUB * n].rearrange("p (s d) -> p s d", s=SUB)

        def tail_load(sp, dst, src, s=tail_in):
            sp.dma_start(dst, src).then_inc(s, 16)

        def load_sums(sp, c):
            tail_load(sp, acc[:, :, :], a_dram[c, :, :, :], acc_in)
            tail_load(sp, xr[:, :, :], x[ds(c * CH, CH), :].rearrange("(s p) d -> p s d", p=P), acc_in)

        def tail_parameters(sp):
            for dst, src in ((w1_sb, w1), (w2_sb[:, :, :], w2.rearrange("(m p) d -> p m d", p=P)),
                             (wp_sb, w_proj), (wt_raw[0:HID, :], Wt), (wpr_raw, Wp)):
                tail_load(sp, dst, src)
            for r, v in ((bproj_r, b_proj), (b2_r, b2), (bp_r, bp), (gamma_r, gamma), (beta_r, beta),
                         (bt_r, bt), (wa_r, Wa.rearrange("a b -> (a b)")), (ba_r, ba)):
                tail_load(sp, r, v.rearrange("(a n) -> a n", a=1).to_broadcast([P, v.shape[0]]))
            for m in range(NM):
                tail_load(sp, b1_c[:, m:m + 1], b1[m * P:(m + 1) * P].rearrange("(p a) -> p a", a=1))
            tail_load(sp, g2_c, g2.rearrange("(p a) -> p a", a=1))
            tail_load(sp, be2_c, be2.rearrange("(p a) -> p a", a=1))

        def tail_sync(sp):
            with sp.Fori(1, NC) as c:
                sp.wait_ge(acc_turned, c)
                sp.wait_ge(xb_made, c)
                load_sums(sp, c)
            phase_end(sp, 3)
            layer2_sync(sp)

        N_TAIL_IN = 16 * (15 + NM)

        def tail_gpsimd(pool):
            pool.wait_ge(tail_in, N_TAIL_IN)
            nc.gpsimd.memset(h3[:, :, 3 * HID:], 1.0)

            def input_bias(c):
                pool.wait_ge(acc_in, 32 * c + 32)
                nc.gpsimd.tensor_tensor(xb, xr, per_row(bproj_r), ALU.add).then_inc(xb_made, 1)

            def root(c):
                pool.wait_ge(mv2_made, c + 1)
                nc.gpsimd.tensor_tensor(rstd2, mv2[:, :, 1], cols[:, 9:10].to_broadcast([P, SUB]), ALU.add)\
                    .then_inc(eps2_added, 1)
                pool.wait_ge(eps2_added, c + 1)
                nc.gpsimd.tensor_tensor(rstd2, rstd2, cols[:, 8:9].to_broadcast([P, SUB]), ALU.pow)\
                    .then_inc(rstd2_made, 1)

            def x1_bias():
                nc.gpsimd.tensor_tensor(x1b, x1, per_row(b2_r), ALU.add).then_inc(x1b_made, 1)

            def x2_bias(c):
                pool.wait_ge(x2_made, c + 1)
                nc.gpsimd.tensor_tensor(x2_sb[:, ds(c * SUB, SUB), :], x2, per_row(bp_r), ALU.add)\
                    .then_inc(x2b_made, 1)

            input_bias(0)
            root(0)
            x1_bias()
            with pool.Fori(0, NC - 1) as c:
                input_bias(c + 1)
                root(c + 1)
                x2_bias(c)
                x1_bias()
            x2_bias(NC - 1)
            phase_end(pool, 3)
            layer2_gpsimd(pool)

        def tail_scalar(act):
            act.wait_ge(tail_in, N_TAIL_IN)
            act.wait_ge(wT_turned, 1)
            nc.scalar.activation(wtT, ps[:, 0, 0:HID], ACT.Copy)
            nc.scalar.activation(wpT[0:HID, :], ps[0:HID, 1, 0:D], ACT.Copy).then_inc(wT_copied, 1)

            def turned_att(c):
                act.wait_ge(att_turned, c + 1)
                nc.scalar.activation(attT, ps[:, B_TURN, :], ACT.Copy).then_inc(attT_made, 1)

            def turned_h2(c):
                act.wait_ge(h2_turned, c + 1)
                nc.scalar.activation(h2T, ps[:, B_TURN, :], ACT.Identity, bias=be2_c, scale=g2_c)\
                    .then_inc(h2T_made, 1)

            def gelu(c, m):
                act.wait_ge(ff1_done, NM * c + m + 1)
                nc.scalar.activation(ff[:, m, :], ps[:, B_FF + m, :], ACT.Gelu_apprx_tanh,
                                     bias=b1_c[:, m:m + 1]).then_inc(gelu_made, 1)

            def turned_x2(c):
                act.wait_ge(x2_turned, c + 1)
                nc.scalar.activation(x2T, ps[:, B_X2, :], ACT.Copy).then_inc(x2T_made, 1)

            def step(c, first, last):
                gelu(c, 0)
                gelu(c, 1)
                if not last:
                    turned_att(c + 1)
                gelu(c, 2)
                if not first:
                    turned_x2(c - 1)
                gelu(c, 3)
                if not last:
                    turned_h2(c + 1)

            turned_att(0)
            turned_h2(0)
            step(0, True, False)
            if NC > 2:
                with act.Fori(1, NC - 1) as c:
                    step(c, False, False)
            step(NC - 1, False, True)
            turned_x2(NC - 1)
            phase_end(act, 3)
            layer2_scalar(act)

        def tail_vector(dve):
            dve.wait_ge(tail_in, N_TAIL_IN)

            def normalise_att(c):
                t = ps[:, B_ACC:B_ACC + 2, :].rearrange("p g (s h k) -> p g s h k", s=SUB, h=HG)
                r = rl.rearrange("p (g s h) -> p g s h", g=2, s=SUB)
                dve.wait_ge(acc_turned, c + 1)
                nc.vector.reciprocal(rl.rearrange("p (a h) -> p a h", h=HG),
                                     t[:, :, :, :, HD].rearrange("p g s h -> p (g s) h")).then_inc(rl_made, 1)
                dve.wait_ge(rl_made, c + 1)
                a = att.rearrange("p (s g h) d -> p s g h d", s=SUB, g=2)
                for g in range(2):
                    last = nc.vector.tensor_tensor(
                        a[:, :, g, :, :], t[:, g, :, :, 0:HD],
                        r[:, g, :, :].rearrange("p s (h a) -> p s h a", a=1).to_broadcast([P, SUB, HG, HD]),
                        ALU.mult)
                last.then_inc(att_made, 1)

            def first_sum(c):
                dve.wait_ge(projected, c + 1)
                dve.wait_ge(xb_made, c + 1)
                nc.vector.tensor_tensor(x1, by_tile(B_PROJ), xb, ALU.add).then_inc(x1_made, 1)
                dve.wait_ge(x1_made, c + 1)
                for s in range(SUB):
                    last = nc.vector.bn_stats(bn2[:, s, :], x1[:, s, :])
                last.then_inc(bn2_made, 1)
                dve.wait_ge(bn2_made, c + 1)
                settle(dve)
                for s in range(SUB):
                    last = nc.vector.bn_aggr(mv2[:, s, :], bn2[:, s, :])
                last.then_inc(mv2_made, 1)

            def normalise_x1(c):
                dve.wait_ge(rstd2_made, c + 1)
                for s in range(SUB):
                    last = nc.vector.tensor_scalar(h2[:, s, :], x1[:, s, :], mv2[:, s, 0:1],
                                                   rstd2[:, s:s + 1], ALU.subtract, ALU.mult)
                last.then_inc(h2_made, 1)

            def second_sum(c):
                dve.wait_ge(ff2_done, c + 1)
                dve.wait_ge(x1b_made, c + 1)
                nc.vector.tensor_tensor(x2, by_tile(B_OUT), x1b, ALU.add).then_inc(x2_made, 1)

            def hidden(c):
                dve.wait_ge(hid_done, c + 1)
                nc.vector.tensor_tensor(hid, by_tile(B_HID, HID), per_row(bt_r, HID), ALU.add)\
                    .then_inc(hid_made, 1)

            def hidden_parts(c):
                at = ds(c * SUB, SUB)
                dve.wait_ge(hid_made, c + 1)
                nc.vector.tensor_copy(h3[:, at, 0:HID], hid).then_inc(hid_step, 1)
                dve.wait_ge(hid_step, 8 * c + 1)
                nc.vector.tensor_tensor(rest_h, hid, h3[:, at, 0:HID], ALU.subtract).then_inc(hid_step, 1)
                dve.wait_ge(hid_step, 8 * c + 2)
                nc.vector.tensor_copy(h3[:, at, HID:2 * HID], rest_h).then_inc(hid_step, 1)
                dve.wait_ge(hid_step, 8 * c + 3)
                nc.vector.tensor_tensor(h3[:, at, 2 * HID:3 * HID], rest_h, h3[:, at, HID:2 * HID],
                                        ALU.subtract).then_inc(hid_step, 1)
                dve.wait_ge(hid_step, 8 * c + 4)
                nc.vector.tensor_tensor(rest_h, hid, per_row(wa_r, HID), ALU.mult).then_inc(hid_step, 1)
                dve.wait_ge(hid_step, 8 * c + 5)
                nc.vector.tensor_reduce(s_row[:, at], rest_h, AX.X, ALU.add).then_inc(hid_step, 1)
                dve.wait_ge(hid_step, 8 * c + 6)
                nc.vector.tensor_scalar(s_row[:, at], s_row[:, at], ba_r, None, ALU.add).then_inc(hid_step, 1)
                dve.wait_ge(hid_step, 8 * c + 7)
                nc.vector.scalar_tensor_tensor(out=s_row[:, at], in0=s_row[:, at], scalar=0.2,
                                               in1=s_row[:, at], op0=ALU.mult, op1=ALU.max)\
                    .then_inc(hid_step, 1)

            def step(c, first, last):
                if not last:
                    normalise_att(c + 1)
                    first_sum(c + 1)
                if not first:
                    hidden(c - 1)
                if not last:
                    normalise_x1(c + 1)
                second_sum(c)
                if not first:
                    hidden_parts(c - 1)

            normalise_att(0)
            first_sum(0)
            normalise_x1(0)
            step(0, True, False)
            if NC > 2:
                with dve.Fori(1, NC - 1) as c:
                    step(c, False, False)
            step(NC - 1, False, True)
            hidden(NC - 1)
            hidden_parts(NC - 1)
            phase_end(dve, 3)
            layer2_vector(dve)

        def tail_tensor(pe):
            pe.wait_ge(tail_in, N_TAIL_IN)
            nc.tensor.transpose(ps[:, 0, 0:HID], wt_raw[0:HID, :], identf[0:HID, 0:HID])
            nc.tensor.transpose(ps[0:HID, 1, 0:D], wpr_raw, identf[:, :]).then_inc(wT_turned, 1)
            pe.wait_ge(wT_copied, 1)

            def turn_acc(c, after_hidden=False):
                pe.wait_ge(acc_in, 32 * c + 32)
                if after_hidden:
                    pe.wait_ge(hid_made, c - 2)
                for g in range(2):
                    for s in range(SUB):
                        last = nc.tensor.transpose(ps[:, B_ACC + g, s * P:(s + 1) * P],
                                                   acc[:, g, s * P:(s + 1) * P], identf[:, :])
                last.then_inc(acc_turned, 1)

            def turn_att(c):
                pe.wait_ge(att_made, c + 1)
                for s in range(SUB):
                    last = nc.tensor.transpose(ps[:, B_TURN, s * P:(s + 1) * P],
                                               att[:, s * H:(s + 1) * H, :].rearrange("p h d -> p (h d)"),
                                               identf[:, :])
                last.then_inc(att_turned, 1)

            def project(c):
                pe.wait_ge(attT_made, c + 1)
                for s in range(SUB):
                    last = nc.tensor.matmul(ps[:, B_PROJ, s * D:(s + 1) * D], attT[:, s * P:(s + 1) * P],
                                            wp_sb, start=True, stop=True)
                last.then_inc(projected, 1)

            def turn_rows(src, bank, made, turned, c):
                pe.wait_ge(made, c + 1)
                for s in range(SUB):
                    last = nc.tensor.transpose(ps[:, bank, s * P:(s + 1) * P], src[:, s, :], identf[:, :])
                last.then_inc(turned, 1)

            def ff1(c, ms):
                if ms[0] == 0:
                    pe.wait_ge(h2T_made, c + 1)
                for m in ms:
                    nc.tensor.matmul(ps[:, B_FF + m, :], w1_sb[:, m * P:(m + 1) * P], h2T,
                                     start=True, stop=True).then_inc(ff1_done, 1)

            def ff2(c):
                pe.wait_ge(gelu_made, NM * c + NM)
                for s in range(SUB):
                    for m in range(NM):
                        last = nc.tensor.matmul(ps[:, B_OUT, s * D:(s + 1) * D],
                                                ff[:, m, s * P:(s + 1) * P], w2_sb[:, m, :],
                                                start=m == 0, stop=m == NM - 1)
                last.then_inc(ff2_done, 1)

            def hidden(c):
                pe.wait_ge(x2T_made, c + 1)
                for s in range(SUB):
                    last = nc.tensor.matmul(ps[:, B_HID, s * HID:(s + 1) * HID],
                                            x2T[:, s * P:(s + 1) * P], wtT, start=True, stop=True)
                last.then_inc(hid_done, 1)

            def step(c, first, last, ahead):
                ff1(c, (0, 1))
                if not last:
                    turn_att(c + 1)
                if not first:
                    turn_rows(x2, B_X2, x2_made, x2_turned, c - 1)
                ff1(c, (2, 3))
                if not last:
                    project(c + 1)
                if not first:
                    hidden(c - 1)
                ff2(c)
                if not last:
                    turn_rows(h2, B_TURN, h2_made, h2_turned, c + 1)
                if ahead:
                    turn_acc(c + 2, not first)

            turn_acc(0)
            turn_att(0)
            project(0)
            turn_rows(h2, B_TURN, h2_made, h2_turned, 0)
            turn_acc(1)
            step(0, True, False, NC > 2)
            if NC > 3:
                with pe.Fori(1, NC - 2) as c:
                    step(c, False, False, True)
            if NC > 2:
                step(NC - 2, False, False, False)
            step(NC - 1, False, True, False)
            turn_rows(x2, B_X2, x2_made, x2_turned, NC - 1)
            hidden(NC - 1)
            phase_end(pe, 3)
            layer2_tensor(pe)

        AGG = 3 * HID + 1
        HC = CH // 2
        ACT_TILES = NT // 4
        nlo, nsum, den, aw, ew = wb(SUB, HID), wb(SUB, HID), wb(SUB), wb(SUB), wb(SUB)
        wc, nbT, y, y_out = wb(SUB, HID), wb(CH), wb(SUB, D), wb(SUB, D)
        ybn, ymv, yrs = wb(SUB, 6), wb(SUB, 2), wb(SUB)
        B_NB, B_Y, B_ONES = 4, 5, 5

        edges_in = [[sem(f"edges_in{u}{half}") for half in range(2)] for u in range(2)]
        edges_made = sem("edges_made")
        edges_used = sem("edges_used")
        ones_done = sem("ones_done")
        row_step = sem("row_step")
        e_made = sem("e_made")
        lo_copied = sem("lo_copied")
        agg_read = sem("agg_read")
        den_step = sem("den_step")
        wc_made = sem("wc_made")
        nb_made = sem("nb_made")
        nb_turned = sem("nb_turned")
        nbT_made = sem("nbT_made")
        y_done = sem("y_done")
        y_step = sem("y_step")
        yr_step = sem("yr_step")
        y_normed = sem("y_normed")
        scaled = sem("scaled")
        edges_by_act = sem("edges_by_act")
        out_made = sem("out_made")
        out_stored = sem("out_stored")

        def sums(u):
            return ps[:, 2 * u:2 * u + 2, :].rearrange("p b (h n) -> p (b h) n", h=2)

        def layer2_sync(sp):
            def loads(j, u):
                for half in range(2):
                    q = slice(half * HC, (half + 1) * HC)
                    sp.wait_ge(edges_used, 2 * (j - 2) + half + 1)
                    settle(sp)
                    sp.dma_start(m_view[:, (j + 1) % 2, :, q], m_dram[NC - 1 - j, :, :, q])\
                        .then_inc(edges_in[u][half], 16)

            if NC > 2:
                with sp.Fori(1, NC // 2) as i:
                    for u in range(2):
                        loads(2 * i + u, u)
            sp.wait_ge(out_stored, 16 * (NC + 1))

        def layer2_gpsimd(pool):
            with pool.Fori(0, NC) as j:
                pool.wait_ge(y_step, 3 * j + 3)
                nc.gpsimd.tensor_tensor(yrs, ymv[:, :, 1], cols[:, 9:10].to_broadcast([P, SUB]), ALU.add)\
                    .then_inc(yr_step, 1)
                pool.wait_ge(yr_step, 2 * j + 1)
                nc.gpsimd.tensor_tensor(yrs, yrs, cols[:, 8:9].to_broadcast([P, SUB]), ALU.pow)\
                    .then_inc(yr_step, 1)
                pool.wait_ge(y_normed, j + 1)
                pool.wait_ge(out_stored, 16 * j + 16)
                nc.gpsimd.tensor_tensor(y_out, y, per_row(gamma_r), ALU.mult).then_inc(scaled, 1)
                pool.wait_ge(scaled, j + 1)
                nc.gpsimd.tensor_tensor(y_out, y_out, per_row(beta_r), ALU.add).then_inc(out_made, 1)

        def layer2_scalar(act):
            def edge_half(j, half):
                e = m_view[:, (j + 1) % 2, NT - ACT_TILES:, half * HC:(half + 1) * HC]
                nc.scalar.activation(e, e, ACT.Copy, scale=1.0 / HUGE, bias=1.0).then_inc(edges_by_act, 1)

            for j in range(2):
                for half in range(2):
                    edge_half(j, half)
            act.wait_ge(row_step, 3)
            nc.scalar.activation(e1, e1, ACT.Exp)
            nc.scalar.activation(e0, e0, ACT.Exp).then_inc(e_made, 1)
            act.wait_ge(e_made, 1)

            act.sem_inc(out_stored, 16)

            def step(j, u, i, first):
                act.wait_ge(edges_used, 2 * j + 2)
                act.wait_ge(agg_read, j + 1)
                nc.scalar.activation(nlo, sums(u)[:, :, 2 * HID:3 * HID], ACT.Copy).then_inc(lo_copied, 1)
                act.wait_ge(nb_turned, j + 1)
                nc.scalar.activation(nbT[0:HID, :], ps[0:HID, B_NB, :], ACT.Copy).then_inc(nbT_made, 1)
                if i is not None:
                    act.wait_ge(edges_in[u][0], 16 * i + 16)
                    edge_half(j + 2, 0)
                if not first:
                    store(j - 1)
                if i is not None:
                    act.wait_ge(edges_in[u][1], 16 * i + 16)
                    edge_half(j + 2, 1)

            def store(j):
                act.wait_ge(out_made, j + 1)
                settle(act)
                o = out[ds((NC - 1 - j) * CH, CH), :].rearrange("(s p) d -> p s d", p=P)
                act.dma_start(o, y_out[:, :, :]).then_inc(out_stored, 16)

            more = NC > 2
            for u in range(2):
                step(u, u, 0 if more else None, u == 0)
            if NC > 4:
                with act.Fori(1, NC // 2 - 1) as i:
                    for u in range(2):
                        step(2 * i + u, u, i, False)
            if more:
                for u in range(2):
                    step(NC - 2 + u, u, None, False)
            store(NC - 1)

        def layer2_vector(dve):
            dve.sem_inc(agg_read, 1)

            def edge_half(j, half, i=None, u=None):
                if i is not None:
                    dve.wait_ge(edges_in[u][half], 16 * i + 16)
                e = m_view[:, (j + 1) % 2, 0:NT - ACT_TILES, half * HC:(half + 1) * HC]
                nc.vector.tensor_scalar(e, e, 0.0, None, ALU.is_ge).then_inc(edges_made, 1)

            for j in range(2):
                for half in range(2):
                    edge_half(j, half)
            dve.wait_ge(ones_done, 1)
            nc.vector.tensor_copy(csum, ps[:, B_ONES, 2 * HID:3 * HID]).then_inc(row_step, 1)
            nc.vector.tensor_scalar(mx, s_row, NEG, None, ALU.max).then_inc(row_step, 1)
            dve.wait_ge(row_step, 2)
            nc.vector.tensor_tensor(csum, csum, ps[:, B_ONES, HID:2 * HID], ALU.add)
            nc.vector.tensor_tensor(e1, s_row, mx, ALU.subtract)
            nc.vector.tensor_scalar(e0, mx, -1.0, NEG, ALU.mult, ALU.add).then_inc(row_step, 1)
            dve.wait_ge(row_step, 3)
            nc.vector.tensor_tensor(csum, csum, ps[:, B_ONES, 0:HID], ALU.add).then_inc(row_step, 1)
            dve.wait_ge(e_made, 1)
            nc.vector.tensor_tensor(e1, e1, e0, ALU.subtract).then_inc(row_step, 1)
            dve.wait_ge(row_step, 5)

            def read_sums(j, u):
                dve.wait_ge(lo_copied, j + 1)
                s = sums(u)
                nc.vector.tensor_tensor(nsum, s[:, :, HID:2 * HID], nlo, ALU.add)
                nc.vector.tensor_tensor(den, s[:, :, 3 * HID], e1[:, ds((NC - 1 - j) * SUB, SUB)], ALU.mult)\
                    .then_inc(den_step, 1)
                dve.wait_ge(den_step, 4 * j + 1)
                nc.vector.tensor_tensor(nsum, s[:, :, 0:HID], nsum, ALU.add).then_inc(agg_read, 1)

            def wide(v, n):
                return v.rearrange("p (s a) -> p s a", a=1).to_broadcast([P, SUB, n])

            def neighbours(j):
                at = ds((NC - 1 - j) * SUB, SUB)
                nc.vector.scalar_tensor_tensor(out=den, in0=e0[:, at], scalar=float(N), in1=den,
                                               op0=ALU.mult, op1=ALU.add).then_inc(den_step, 1)
                dve.wait_ge(den_step, 4 * j + 2)
                nc.vector.reciprocal(den, den).then_inc(den_step, 1)
                dve.wait_ge(den_step, 4 * j + 3)
                nc.vector.tensor_tensor(aw, e1[:, at], den, ALU.mult)
                nc.vector.tensor_tensor(ew, e0[:, at], den, ALU.mult).then_inc(den_step, 1)
                dve.wait_ge(den_step, 4 * j + 4)
                dve.wait_ge(agg_read, j + 1 + 1)
                nc.vector.tensor_tensor(nsum, nsum, wide(aw, HID), ALU.mult)
                nc.vector.tensor_tensor(wc, per_row(csum, HID), wide(ew, HID), ALU.mult).then_inc(wc_made, 1)
                dve.wait_ge(wc_made, j + 1)
                nc.vector.tensor_tensor(nsum, nsum, wc, ALU.add).then_inc(nb_made, 1)

            def residual(j, first=False):
                dve.wait_ge(y_done, j + 1)
                if not first:
                    dve.wait_ge(scaled, j)
                nc.vector.tensor_tensor(y, by_tile(B_Y), x2_sb[:, ds((NC - 1 - j) * SUB, SUB), :], ALU.add)\
                    .then_inc(y_step, 1)
                dve.wait_ge(y_step, 3 * j + 1)
                for s in range(SUB):
                    last = nc.vector.bn_stats(ybn[:, s, :], y[:, s, :])
                last.then_inc(y_step, 1)
                dve.wait_ge(y_step, 3 * j + 2)
                settle(dve)
                for s in range(SUB):
                    last = nc.vector.bn_aggr(ymv[:, s, :], ybn[:, s, :])
                last.then_inc(y_step, 1)

            def finish(j):
                dve.wait_ge(yr_step, 2 * j + 2)
                for s in range(SUB):
                    last = nc.vector.tensor_scalar(y[:, s, :], y[:, s, :], ymv[:, s, 0:1], yrs[:, s:s + 1],
                                                   ALU.subtract, ALU.mult)
                last.then_inc(y_normed, 1)

            def step(j, u, i, first):
                read_sums(j, u)
                neighbours(j)
                if i is not None:
                    edge_half(j + 2, 0, i, u)
                residual(j, first)
                if i is not None:
                    edge_half(j + 2, 1, i, u)
                finish(j)

            more = NC > 2
            for u in range(2):
                step(u, u, 0 if more else None, u == 0)
            if NC > 4:
                with dve.Fori(1, NC // 2 - 1) as i:
                    for u in range(2):
                        step(2 * i + u, u, i, False)
            if more:
                for u in range(2):
                    step(NC - 2 + u, u, None, False)

        def layer2_tensor(pe):
            pe.wait_ge(edges_made, 1)
            for t in range(NT):
                last = nc.tensor.matmul(ps[:, B_ONES, 0:AGG], ones_b[:, :], h3[:, t, 0:AGG],
                                        start=t == 0, stop=t == NT - 1)
            last.then_inc(ones_done, 1)

            def aggregate(j, u, rows):
                for s in rows:
                    if s % 2 == 0:
                        pe.wait_ge(edges_made, 2 * j + s // 2 + 1)
                        pe.wait_ge(edges_by_act, 2 * j + s // 2 + 1)
                    for t in range(NT):
                        last = nc.tensor.matmul(sums(u)[:, s, 0:AGG],
                                                m_view[:, (u + 1) % 2, t, s * P:(s + 1) * P], h3[:, t, 0:AGG],
                                                start=t == 0, stop=t == NT - 1)
                    if s % 2:
                        last.then_inc(edges_used, 1)

            def turn_neighbours(j):
                pe.wait_ge(nb_made, j + 1)
                settle(pe)
                for s in range(SUB):
                    last = nc.tensor.transpose(ps[0:HID, B_NB, s * P:(s + 1) * P], nsum[:, s, :], identf[:, :])
                last.then_inc(nb_turned, 1)

            def project(j):
                pe.wait_ge(nbT_made, j + 1)
                for s in range(SUB):
                    last = nc.tensor.matmul(ps[:, B_Y, s * D:(s + 1) * D], nbT[0:HID, s * P:(s + 1) * P],
                                            wpT[0:HID, :], start=True, stop=True)
                last.then_inc(y_done, 1)

            def step(j, u, first):
                aggregate(j, u, (0, 1))
                if not first:
                    turn_neighbours(j - 1)
                aggregate(j, u, (2,))
                if not first:
                    project(j - 1)
                aggregate(j, u, (3,))

            step(0, 0, True)
            step(1, 1, False)
            if NC > 2:
                with pe.Fori(1, NC // 2) as i:
                    for u in range(2):
                        step(2 * i + u, u, False)
            turn_neighbours(NC - 1)
            project(NC - 1)

        block = ctx.enter_context(nc.Block())

        gm_words = mask_t[:, NT * CH:2 * NT * CH].bitcast(F32)
        gm_adj = gm_words[:, 0:N].bitcast(I32)
        gm_mask = gm_words[:, N:N + N // 2].bitcast(BF16)
        gm_q = q_pack[:, 0, :, :].rearrange("p h q -> p (h q)")[:, 0:H * P].rearrange("p (h q) -> p h q", h=H)
        gm_s = pool_words[:, 0:N]
        gm_c = pool_words[:, N:N + 2 * H].rearrange("p (a h) -> p a h", h=H)
        gm_c3 = pool_words[:, N + 2 * H:N + 4 * H].bitcast(BF16)[:, 0:3 * H].rearrange("p (a h) -> p a h", h=H)
        gm_ct = pool_words[:, N + 4 * H:N + 4 * H + P // 2].bitcast(BF16)
        gm_loaded = sem("gm_loaded")
        gm_converted = sem("gm_converted")
        gm_scored = sem("gm_scored")
        gm_masked = sem("gm_masked")
        gm_maxed = sem("gm_maxed")
        gm_split = sem("gm_split")
        gm_turned = sem("gm_turned")
        gm_copied = sem("gm_copied")
        gm_stored = sem("gm_stored")
        gm_phase = sem("gm_phase")

        def exact_maximum(eng, program):
            eng.wait_ge(flag_made, 3)
            too_large = eng.value_load(flag[0:1, 0:1], min_val=0, max_val=1)
            with eng.If(too_large > 0):
                program(eng)
                eng.drain().then_inc(gm_phase, 1)
                eng.wait_ge(gm_phase, 5)
                settle(eng)

        def maximum_sync(sp):
            sp.sem_inc(gm_stored, 16)
            with sp.Fori(0, NT) as T:
                sp.wait_ge(gm_stored, 16 * T + 16)
                sp.dma_start(gm_adj, adj[ds(T * P, P), :]).then_inc(gm_loaded, 16)
                sp.dma_start(gm_q[0:KW, :, :], q_dram[T, :, :, :]).then_inc(gm_loaded, 16)
                sp.wait_ge(gm_copied, T + 1)
                sp.dma_start(q_dram[T, PARTS:KW, :, :].rearrange("k h q -> (k h) q"), gm_ct[0:3 * H, :])\
                    .then_inc(gm_stored, 16)
            sp.wait_ge(gm_stored, 16 * NT + 16)

        def maximum_none(eng):
            eng.sem_inc(settled, 1)

        def maximum_vector(dve):
            dve.sem_inc(gm_maxed, 1)
            with dve.Fori(0, NT) as T:
                dve.wait_ge(gm_loaded, 32 * T + 32)
                nc.vector.tensor_scalar(gm_mask, gm_adj, 0.0, -HUGE, ALU.is_equal, ALU.mult)\
                    .then_inc(gm_converted, 1)
                dve.wait_ge(gm_converted, T + 1)
                settle(dve)
                with dve.Fori(0, H) as h:
                    n = T * H + h
                    dve.wait_ge(gm_scored, n + 1)
                    dve.wait_ge(gm_maxed, n + 1)
                    nc.vector.tensor_tensor(gm_s, ps[:, 0:NC, :].rearrange("p b n -> p (b n)"), gm_mask,
                                            ALU.add).then_inc(gm_masked, 1)
                    dve.wait_ge(gm_masked, n + 1)
                    nc.vector.tensor_reduce(gm_c[:, 0, ds(h, 1)], gm_s, AX.X, ALU.max, negate=True)\
                        .then_inc(gm_maxed, 1)
                dve.wait_ge(gm_maxed, T * H + H + 1)
                settle(dve)
                nc.vector.tensor_copy(gm_c3[:, 0, :], gm_c[:, 0, :]).then_inc(gm_split, 1)
                dve.wait_ge(gm_split, 4 * T + 1)
                nc.vector.tensor_tensor(gm_c[:, 1, :], gm_c[:, 0, :], gm_c3[:, 0, :], ALU.subtract)\
                    .then_inc(gm_split, 1)
                dve.wait_ge(gm_split, 4 * T + 2)
                nc.vector.tensor_copy(gm_c3[:, 1, :], gm_c[:, 1, :]).then_inc(gm_split, 1)
                dve.wait_ge(gm_split, 4 * T + 3)
                nc.vector.tensor_tensor(gm_c3[:, 2, :], gm_c[:, 1, :], gm_c3[:, 1, :], ALU.subtract)\
                    .then_inc(gm_split, 1)
                dve.wait_ge(gm_turned, T + 1)
                nc.vector.tensor_copy(gm_ct[0:3 * H, :], bank16[0][0:3 * H, 0:P]).then_inc(gm_copied, 1)

        def maximum_tensor(pe):
            with pe.Fori(0, NT) as T:
                pe.wait_ge(gm_loaded, 32 * T + 32)
                settle(pe)
                with pe.Fori(0, H) as h:
                    pe.wait_ge(gm_maxed, T * H + h + 1)
                    for kb in range(NC):
                        last = nc.tensor.matmul(ps[:, kb, :], gm_q[0:KW, h, :],
                                                k_view[0:KW, h, kb * CH:(kb + 1) * CH], start=True, stop=True)
                    last.then_inc(gm_scored, 1)
                pe.wait_ge(gm_split, 4 * T + 4)
                settle(pe)
                nc.tensor.transpose(bank16[0][0:3 * H, 0:P], gm_c3.rearrange("p a h -> p (a h)"), ident[:, :])\
                    .then_inc(gm_turned, 1)

        def settle(eng):
            eng.sem_inc(settled, 1)

        def phase_end(eng, n):
            eng.drain().then_inc(phase, 1)
            eng.wait_ge(phase, 5 * n)

        @block.sync
        def _(sp):
            def load_adj(X):
                sp.wait_ge(converted, X + ONE)
                sp.wait_ge(mask_stored, 16 * X + 16)
                c, i = (X % (NC * MB)) // MB, X % MB
                src = adj[ds(c * CH, CH), ds(i * 2 * P, 2 * P)].rearrange("(s p) k -> p s k", p=P)
                sp.dma_start(adj_in[:, :, :], src).then_inc(adj_loaded, 16)

            def store_mask(X, c, i, slot):
                sp.wait_ge(evacuated, 2 * X + 2 + TP)
                src = m_view[:, slot, ds(2 * i, 2), :]
                sp.dma_start(m_dram[c, :, ds(2 * i, 2), :], src).then_inc(mask_stored, 16)

            def store_q(T, u):
                sp.wait_ge(q_out_made, T + 1 + ONE)
                sp.dma_start(q_dram[T, :, :, :], q_out[0:KW, u, :, :]).then_inc(q_stored[u], 16)

            def store_v(T, u):
                sp.wait_ge(hi_made, T + 1 + 2)
                sp.dma_start(v_dram[:, T, :, :].rearrange("g p k -> p g k"),
                             v_out[:, u, :, :].rearrange("p (g h) k -> p g (h k)", g=2))\
                    .then_inc(v_stored[u], 16)

            sp.sem_inc(mask_stored, 32)
            for u in range(RING):
                sp.sem_inc(q_stored[u], 16)
                sp.sem_inc(v_stored[u], 16)
            for g in range(2):
                sp.sem_inc(acc_stored[g], 16)
            xv = x.rearrange("(t p) d -> p t d", p=P)
            for j in range(4):
                w = NT // 4
                sp.dma_start(x_sb[:, j * w:(j + 1) * w, :], xv[:, j * w:(j + 1) * w, :]).then_inc(x_in[j], 16)
            sp.dma_start(wqkv, w_qkv).then_inc(params_in, 16)
            for k, v in enumerate((g1, be1)):
                sp.dma_start(cols[:, k:k + 1], v.rearrange("(p a) -> p a", a=1)).then_inc(params_in, 16)

            load_adj(0)
            for u in range(2):
                store_v(u, u)

            def steps_of(i, last):
                for u in range(RING):
                    T, X = RING * i + u, 2 * i + u // 2
                    if u % 2 == 0:
                        load_adj(X + 1)
                    if not (last and u + 2 >= RING):
                        store_v(T + 2, (u + 2) % RING)
                    store_q(T, u)
                    if u % 2:
                        store_mask(X, 0, X, 0)
            with sp.Fori(0, NT // RING - 1) as i:
                steps_of(i, False)
            steps_of(NT // RING - 1, True)
            for u in range(RING):
                sp.wait_ge(q_stored[u], 16 * (NT // RING + 1))
                sp.wait_ge(v_stored[u], 16 * (NT // RING + 1))
            phase_end(sp, 1)
            exact_maximum(sp, maximum_sync)

            def load_q(c, g):
                for hh in range(HG):
                    src = q_dram[ds(c * SUB, SUB), :, g * HG + hh, :].rearrange("s k q -> k s q")
                    sp.dma_start(q_pack[0:KW, g, hh, :].rearrange("k (s q) -> k s q", q=P), src)\
                        .then_inc(q_loaded[g], 16)

            def load_v(BI, h):
                sp.wait_ge(pv_done, 4 * BI + 2 * h + 2)
                b, g = BI % NB, (BI // NB) % 2
                src = v_dram[g, ds(b * SLOTS + 2 * h, 2), :, :]
                sp.dma_start(v_st[:, 2 * h:2 * h + 2, :], src.rearrange("t p k -> p t k"))\
                    .then_inc(v_loaded[h], 16)

            def body(c, g, b, prep):
                BI = (c * 2 + g) * NB + b
                i = b + g * NB
                X = (c + 1) * MB + i
                if prep:
                    load_adj(X + 1)
                load_v(BI + 1, 0)
                if prep:
                    store_mask(X, c + 1, i, (c + 1) % 2)
                load_v(BI + 1, 1)

            def store_acc(c, g):
                sp.wait_ge(acc_copied[g], c + 1 + ONE)
                sp.dma_start(a_dram[c, :, g, :], acc_sb[:, g, :]).then_inc(acc_stored[g], 16)

            def segment(c, g, prep, before):
                if NB > 1:
                    with sp.Fori(0, NB - 1) as b:
                        body(c, g, b, prep)
                body(c, g, NB - 1, prep)
                if before is not None:
                    store_acc(*before)

            load_q(0, 0)
            for h in range(2):
                load_v(0, h)
            load_q(0, 1)
            tail_parameters(sp)

            def chunk(c, prep, first):
                segment(c, 0, prep, None if first else (c - 1, 1))
                if prep:
                    sp.wait_ge(scored, (2 * c + 1) * SEG_UNITS)
                    load_q(c + 1, 0)
                segment(c, 1, prep, (c, 0))
                if prep:
                    sp.wait_ge(scored, (2 * c + 2) * SEG_UNITS)
                    load_q(c + 1, 1)

            chunk(0, True, True)
            if NC > 2:
                with sp.Fori(1, NC - 1) as c:
                    chunk(c, True, False)
            chunk(NC - 1, False, False)
            for g in range(2):
                sp.wait_ge(acc_stored[g], 16 * NC)
            load_sums(sp, 0)
            store_acc(NC - 1, 1)
            for g in range(2):
                sp.wait_ge(acc_stored[g], 16 * (NC + 1))
                sp.wait_ge(v_loaded[g], 16 * (2 * NC * NB + 1))
            sp.wait_ge(adj_loaded, 16 * (NC * MB + 1))
            sp.wait_ge(mask_stored, 16 * (NC * MB + 2))
            phase_end(sp, 2)
            tail_sync(sp)

        @block.gpsimd
        def _(pool):
            pool.sem_inc(sq_made, RING)
            nc.gpsimd.memset(ident[:, :], 0.0)
            nc.gpsimd.memset(ones_b[:, :], 1.0)
            nc.gpsimd.memset(identf[:, :], 0.0)
            nc.gpsimd.memset(zeros[:, :], 0.0)
            nc.gpsimd.memset(cols[:, 8:9], -0.5)
            nc.gpsimd.memset(cols[:, 9:10], EPS)
            nc.gpsimd.memset(v_out[:, :, :, HD:VW], 1.0)
            nc.gpsimd.memset(packed[:, :, 0:H, PARTS:KW], 0.0)
            nc.gpsimd.memset(packed[:, :, H:2 * H, PARTS:KW], 1.0).then_inc(ident_zeroed, 1)
            pool.wait_ge(ident_zeroed, 1)
            for m in (ident, identf):
                last = nc.gpsimd.affine_select(out=m[:, :], in_=m[:, :], compare_op=ALU.not_equal, fill=1.0,
                                               base=0, pattern=[[-1, P]], channel_multiplier=1)
            last.then_inc(const_made, 1)
            pool.wait_ge(const_made, 1)
            w = NT // 4
            for j in range(4):
                at = slice(j * w, j * w + w)
                pool.wait_ge(var_made, j + 1)
                nc.gpsimd.tensor_scalar(rstd[:, at], mv[:, at, 1], EPS, None, ALU.add).then_inc(eps_added, 1)
                pool.wait_ge(eps_added, j + 1)
                nc.gpsimd.tensor_tensor(rstd[:, at], rstd[:, at], cols[:, 8:9].to_broadcast([P, w]), ALU.pow)\
                    .then_inc(rstd_made, 1)

            def stage1(T, u):
                pool.wait_ge(norms_made, T + 1)
                pool.wait_ge(hi_made, T + 1 + 2)
                nc.gpsimd.tensor_tensor(sq[:, u % 2, :].rearrange("p (h k) -> p h k", k=HD),
                                        packed[:, u, :, 0:HD], packed[:, u, :, 0:HD], ALU.mult)\
                    .then_inc(sq_made, 1)

            with pool.Fori(0, NT // RING) as i:
                for u in range(RING):
                    stage1(RING * i + u, u)
            phase_end(pool, 1)
            pool.wait_ge(bound_step, 1)
            nc.gpsimd.partition_all_reduce(small[:, 1, :], small[:, 0, :], P, bass.bass_isa.ReduceOp.max)\
                .then_inc(bound_step, 1)
            exact_maximum(pool, maximum_none)
            phase_end(pool, 2)
            tail_gpsimd(pool)

        @block.scalar
        def _(act):
            act.sem_inc(hT_made, 2)
            act.sem_inc(hi_made, 2)
            act.sem_inc(q_out_made, ONE)
            act.wait_ge(params_in, 48)

            def norm_turned(T, u):
                act.wait_ge(xT_done, T + 1 + XN)
                act.wait_ge(qkv_done, T + 1)
                nc.scalar.activation(hT[:, u, :], ps[:, u % 2, 0:P], ACT.Identity, bias=cols[:, 1:2],
                                     scale=cols[:, 0:1]).then_inc(hT_made, 1)

            def split(i, T, u):
                q = ps[:, 2 + u % 2, 0:D].rearrange("p (h a k) -> p h a k", h=H, a=1)
                k = ps[:, 2 + u % 2, D:2 * D].rearrange("p (h a k) -> p h a k", h=H, a=1)
                act.wait_ge(qkv_done, T + 1 + RING)
                act.wait_ge(nT_done, T + 1)
                act.wait_ge(sq_made, T + 1)
                act.wait_ge(v_stored[u], 16 * i + 16)
                nc.scalar.activation(packed[:, u, 0:H, 0:48].rearrange("p h (a k) -> p h a k", a=3),
                                     q.to_broadcast([P, H, 3, HD]), ACT.Copy)
                nc.scalar.activation(packed[:, u, H:, 64:96].rearrange("p h (a k) -> p h a k", a=2),
                                     k.to_broadcast([P, H, 2, HD]), ACT.Copy)
                nc.scalar.activation(packed[:, u, H:, 0:HD], k[:, :, 0, :], ACT.Copy)
                nc.scalar.activation(v_out[:, u, :, 0:HD],
                                     ps[:, 2 + u % 2, 2 * D:3 * D].rearrange("p (h k) -> p h k", h=H),
                                     ACT.Copy).then_inc(hi_made, 1)

            def evac_q(i, T, u):
                act.wait_ge(nT_done, T + 1 + RING)
                act.wait_ge(q_stored[u], 16 * i + 16)
                nc.scalar.activation(q_out[0:KW, u, :, :].rearrange("p h q -> p (h q)"),
                                     bank16[4][0:KW, :], ACT.Copy).then_inc(q_out_made, 1)

            for u in range(3):
                norm_turned(u, u)
            for u in range(2):
                split(0, u, u)

            def steps_of(i, last):
                for u in range(RING):
                    T = RING * i + u
                    if not (last and u + 3 >= RING):
                        norm_turned(T + 3, (u + 3) % RING)
                    if not (last and u + 2 >= RING):
                        split(i + (u + 2) // RING, T + 2, (u + 2) % RING)
                    evac_q(i, T, u)
            with act.Fori(0, NT // RING - 1) as i:
                steps_of(i, False)
            steps_of(NT // RING - 1, True)
            phase_end(act, 1)
            exact_maximum(act, maximum_none)

            act.sem_inc(exped, SB2)

            with act.Fori(0, 2 * NC * NB) as BI:
                for k in range(SLOTS):
                    TL = BI * SLOTS + k
                    act.wait_ge(pv_done, TL + 1)
                    for pair in range(2):
                        act.wait_ge(scored, 2 * TL + pair + 1)
                        nc.scalar.activation(probs[:, k, pair, :],
                                             ps[:, 2 * pair:2 * pair + 2, :].rearrange("p a q -> p (a q)"),
                                             ACT.Exp).then_inc(exped, 1)
            phase_end(act, 2)
            tail_scalar(act)

        @block.vector
        def _(dve):
            dve.sem_inc(converted, ONE)
            dve.sem_inc(evacuated, TP)
            dve.sem_inc(r1_made, 2)
            dve.sem_inc(norms_made, 2)
            dve.sem_inc(k_made, 1)
            for g in range(2):
                dve.sem_inc(acc_copied[g], ONE)

            def convert(X):
                dve.wait_ge(adj_loaded, 16 * X + 16)
                dve.wait_ge(turned, 2 * X + TP)
                nc.vector.tensor_scalar(mask_n[:, :, :], adj_in[:, :, :], 0.0, -HUGE, ALU.is_equal, ALU.mult)\
                    .then_inc(converted, 1)

            def evac(X, slot, i, t):
                dve.wait_ge(turned, 2 * X + t + 1 + TP)
                nc.vector.tensor_copy(m_view[:, slot, 2 * i + t, :], bank16[6 + t][:, 0:CH]).then_inc(evacuated, 1)

            w = NT // 4
            for j in range(4):
                dve.wait_ge(x_in[j], 16)
                for t in range(j * w, j * w + w):
                    last = nc.vector.bn_stats(bn[:, t, :], x_sb[:, t, :])
                last.then_inc(bn_made, 1)
                dve.wait_ge(bn_made, j + 1)
                for t in range(j * w, j * w + w):
                    last = nc.vector.bn_aggr(mv[:, t, :], bn[:, t, :])
                last.then_inc(var_made, 1)
            dve.wait_ge(params_in, 48)
            nc.vector.tensor_scalar(wqkv[:, 0:D], wqkv[:, 0:D], SCALE, None, ALU.mult).then_inc(w_scaled, 1)
            dve.wait_ge(rstd_made, 4)

            def normalise(T, u):
                dve.wait_ge(xT_done, T + 1)
                nc.vector.tensor_scalar(xn[:, u % 2, :], x_sb[:, T, :], mv[:, T, 0:1], rstd[:, ds(T, 1)],
                                        ALU.subtract, ALU.mult).then_inc(xn_made, 1)

            def split(T, u):
                dve.wait_ge(hi_made, T + 1 + 2)
                r = r1[:, u % 2, :].rearrange("p (h a k) -> p h a k", k=HD, a=1)
                rq, rk = r[:, 0:H, 0, :], r[:, H:, 0, :]
                nc.vector.tensor_tensor(r[:, :, 0, :], ps[:, 2 + u % 2, 0:2 * D].rearrange("p (h k) -> p h k", k=HD),
                                        packed[:, u, :, 0:HD], ALU.subtract).then_inc(r1_made, 1)
                dve.wait_ge(r1_made, T + 1 + 2)
                nc.vector.tensor_copy(packed[:, u, 0:H, 48:80].rearrange("p h (a k) -> p h a k", a=2),
                                      r[:, 0:H, :, :].to_broadcast([P, H, 2, HD]))
                nc.vector.tensor_copy(packed[:, u, H:, 16:80].rearrange("p h (a k) -> p h a k", a=2)[:, :, :, 0:HD],
                                      r[:, H:, :, :].to_broadcast([P, H, 2, HD])).then_inc(mid_made, 1)
                dve.wait_ge(mid_made, T + 1)
                nc.vector.tensor_tensor(packed[:, u, 0:H, 80:96], rq, packed[:, u, 0:H, 64:80], ALU.subtract)
                nc.vector.tensor_tensor(packed[:, u, H:, 32:48], rk, packed[:, u, H:, 16:32], ALU.subtract)\
                    .then_inc(lo_made, 1)

            def sum_norms(T, u):
                dve.wait_ge(sq_made, T + 1 + RING)
                nc.vector.tensor_reduce(norms[:, T, :], sq[:, u % 2, :].rearrange("p (h k) -> p h k", k=HD),
                                        AX.X, ALU.add).then_inc(norms_made, 1)

            def evac_k(T):
                dve.wait_ge(nT_done, T + 1 + RING)
                nc.vector.tensor_copy(k_view[0:KW, :, ds(T * P, P)],
                                      bank16[5][0:KW, :].rearrange("p (h n) -> p h n", h=H)).then_inc(k_made, 1)

            for u in range(4):
                normalise(u, u)
            for u in range(2):
                split(u, u)
                sum_norms(u, u)

            def steps_of(i, last):
                for u in range(RING):
                    T, X = RING * i + u, 2 * i + u // 2
                    if not last:
                        normalise(T + 4, u)
                    if u % 2 == 0:
                        convert(X)
                    if not (last and u + 2 >= RING):
                        split(T + 2, (u + 2) % RING)
                    evac_k(T)
                    evac(X, 0, X, u % 2)
                    if not (last and u + 2 >= RING):
                        sum_norms(T + 2, (u + 2) % RING)
            with dve.Fori(0, NT // RING - 1) as i:
                steps_of(i, False)
            steps_of(NT // RING - 1, True)
            phase_end(dve, 1)
            nc.vector.tensor_reduce(small[:, 0, :], norms.rearrange("p t k -> p k t"), AX.X, ALU.max)\
                .then_inc(bound_step, 1)
            dve.wait_ge(bound_step, 2)
            nc.vector.tensor_tensor(small[:, 2, 0:H], small[:, 1, 0:H], small[:, 1, H:], ALU.mult)\
                .then_inc(flag_made, 1)
            dve.wait_ge(flag_made, 1)
            nc.vector.tensor_reduce(small[:, 3, 0:1], small[:, 2, 0:H], AX.X, ALU.max).then_inc(flag_made, 1)
            dve.wait_ge(flag_made, 2)
            nc.vector.tensor_scalar(flag[:, 0:1], small[:, 3, 0:1], SAFE * SAFE, None, ALU.is_gt)\
                .then_inc(flag_made, 1)
            exact_maximum(dve, maximum_vector)

            def mask(BI, c, b, k, pair):
                dve.wait_ge(exped, 2 * (BI * SLOTS + k) + pair + 1 + SB2)
                m = m_view[:, c % 2, b * SLOTS + k, :].rearrange("p (a q) -> p a q", a=1)
                pr = probs[:, k, pair, :].rearrange("p (a q) -> p a q", a=2)
                nc.vector.scalar_tensor_tensor(out=pr, in0=m.to_broadcast([P, 2, CH]), scalar=HUGE, in1=pr,
                                               op0=ALU.add, op1=ALU.min).then_inc(masked, 1)

            def body(c, g, b, prep):
                BI = (c * 2 + g) * NB + b
                i = b + g * NB
                X = (c + 1) * MB + i
                for k in range(SLOTS):
                    if prep and k == 1:
                        convert(X)
                    for pair in range(2):
                        if not (k % 2 and pair):
                            mask(BI, c, b, k, pair)
                if prep:
                    for t in range(2):
                        evac(X, (c + 1) % 2, i, t)

            def copy_acc(c, g):
                dve.wait_ge(pv_done, ((2 * c + g) + 1) * NT + SLOTS)
                dve.wait_ge(acc_stored[g], 16 * c + 16)
                nc.vector.tensor_copy(acc_sb[:, g, :], ps[:, 4 + g, :]).then_inc(acc_copied[g], 1)

            def segment(c, g, prep, before):
                if NB > 1:
                    with dve.Fori(0, NB - 1) as b:
                        body(c, g, b, prep)
                body(c, g, NB - 1, prep)
                if before is not None:
                    copy_acc(*before)

            def chunk(c, prep, first):
                dve.wait_ge(evacuated, (c + 1) * 2 * MB + TP)
                settle(dve)
                segment(c, 0, prep, None if first else (c - 1, 1))
                segment(c, 1, prep, (c, 0))

            chunk(0, True, True)
            if NC > 2:
                with dve.Fori(1, NC - 1) as c:
                    chunk(c, True, False)
            chunk(NC - 1, False, False)
            copy_acc(NC - 1, 1)
            phase_end(dve, 2)
            tail_vector(dve)

        @block.tensor
        def _(pe):
            pe.sem_inc(xT_done, XN)
            pe.sem_inc(qkv_done, RING)
            pe.sem_inc(nT_done, RING)
            pe.sem_inc(turned, TP)
            pe.sem_inc(pv_done, SLOTS)
            pe.wait_ge(const_made, 1)
            pe.wait_ge(w_scaled, 1)

            def turn_mask(X, t):
                pe.wait_ge(converted, X + 1 + ONE)
                pe.wait_ge(evacuated, 2 * X + t + 1)
                for s in range(SUB):
                    last = nc.tensor.transpose(bank16[6 + t][:, s * P:(s + 1) * P],
                                               mask_n[:, s, t * P:(t + 1) * P], ident[:, :])
                last.then_inc(turned, 1)

            def turn_x(T, u):
                pe.wait_ge(xn_made, T + 1)
                pe.wait_ge(hT_made, T + 1)
                nc.tensor.transpose(ps[:, u % 2, 0:P], xn[:, u % 2, :], identf[:, :]).then_inc(xT_done, 1)

            def qkv(T, u):
                pe.wait_ge(hT_made, T + 1 + 2)
                pe.wait_ge(hi_made, T + 1)
                pe.wait_ge(r1_made, T + 1)
                nc.tensor.matmul(ps[:, 2 + u % 2, 0:3 * D], hT[:, u, :], wqkv, start=True, stop=True)\
                    .then_inc(qkv_done, 1)

            def turn_packed(T, u):
                pe.wait_ge(lo_made, T + 1)
                pe.wait_ge(k_made, T + 1)
                pe.wait_ge(q_out_made, T + 1)
                for h in range(2 * H):
                    b, j = 4 + h // H, h % H
                    last = nc.tensor.transpose(bank16[b][0:KW, j * P:(j + 1) * P], packed[:, u, h, 0:KW],
                                               ident[:, :])
                last.then_inc(nT_done, 1)

            for u in range(3):
                turn_x(u, u)
            for u in range(2):
                qkv(u, u)

            def steps_of(i, last):
                for u in range(RING):
                    T, X = RING * i + u, 2 * i + u // 2
                    if not (last and u + 3 >= RING):
                        turn_x(T + 3, (u + 3) % RING)
                    if not (last and u + 2 >= RING):
                        qkv(T + 2, (u + 2) % RING)
                    turn_packed(T, u)
                    turn_mask(X, u % 2)
            with pe.Fori(0, NT // RING - 1) as i:
                steps_of(i, False)
            steps_of(NT // RING - 1, True)
            phase_end(pe, 1)
            exact_maximum(pe, maximum_tensor)

            def scores(c, g, b, k, fresh, shifted):
                TL = ((c * 2 + g) * NB + b) * SLOTS + k
                if fresh:
                    pe.wait_ge(q_loaded[g], 64 * c + 64)
                for pair in range(2):
                    by_pe = shifted or (k % 2 and pair)
                    if by_pe:
                        pe.wait_ge(evacuated, c * NT + b * SLOTS + k + 1 + TP)
                    pe.wait_ge(exped, 2 * TL + pair + 1)
                    for j in range(2):
                        hh = 2 * pair + j
                        bank = ps[:, 2 * pair + j, :]
                        kt = k_view[0:KW, g * HG + hh, ds((b * SLOTS + k) * P, P)]
                        last = nc.tensor.matmul(bank, kt, q_pack[0:KW, g, hh, :], start=True, stop=not by_pe)
                        if by_pe:
                            last = nc.tensor.matmul(bank, ident[:, :], m_view[:, c % 2, b * SLOTS + k, :],
                                                    start=False, stop=True)
                    last.then_inc(scored, 1)

            def products(c, g, b, k):
                BI = (c * 2 + g) * NB + b
                if k % 2 == 0:
                    pe.wait_ge(v_loaded[k // 2], 16 * BI + 16)
                pe.wait_ge(masked, 6 * BI + (2, 3, 5, 6)[k])
                if k % 2:
                    pe.wait_ge(exped, 2 * (BI * SLOTS + k) + 2 + SB2)
                for hh in range(HG):
                    last = nc.tensor.matmul(ps[32 * hh:32 * hh + VW, 4 + g, :],
                                            v_st[:, k, hh * VW:(hh + 1) * VW],
                                            probs[:, k, hh // 2, (hh % 2) * CH:(hh % 2 + 1) * CH],
                                            start=False, stop=False, skip_group_check=True)
                last.then_inc(pv_done, 1)

            def clear(c, g):
                pe.wait_ge(acc_copied[g], c + 1)
                nc.tensor.matmul(ps[:, 4 + g, :], zeros[:, 0:P], zeros[:, :], start=True, stop=True,
                                 skip_group_check=True)

            def body(c, g, b, nxt, prep, shifted):
                X = (c + 1) * MB + b + g * NB
                for k in range(SLOTS):
                    ahead = k + LEAD - SLOTS
                    if ahead < 0:
                        scores(c, g, b, k + LEAD, False, shifted)
                    elif nxt is not None:
                        cn, gn, bn_ = nxt
                        scores(cn, gn, bn_, ahead, isinstance(bn_, int) and ahead == 0, shifted)
                    products(c, g, b, k)
                    if prep and k == 1:
                        for t in range(2):
                            turn_mask(X, t)

            def segment(c, g, nxt, prep, shifted):
                clear(c, g)
                if NB > 1:
                    with pe.Fori(0, NB - 1) as b:
                        body(c, g, b, (c, g, b + 1), prep, shifted)
                body(c, g, NB - 1, nxt, prep, shifted)

            def attention(shifted):
                for k in range(LEAD):
                    scores(0, 0, 0, k, k == 0, shifted)
                with pe.Fori(0, NC - 1) as c:
                    segment(c, 0, (c, 1, 0), True, shifted)
                    segment(c, 1, (c + 1, 0, 0), True, shifted)
                segment(NC - 1, 0, (NC - 1, 1, 0), False, shifted)
                segment(NC - 1, 1, None, False, shifted)

            too_large = pe.value_load(flag[0:1, 0:1], min_val=0, max_val=1)
            with pe.If(too_large > 0):
                attention(True)
            with pe.Else():
                attention(False)
            phase_end(pe, 2)
            tail_tensor(pe)


_INS = ["x", "adj", "L0_gnn_w_qkv", "L0_gnn_w_proj", "L0_gnn_b_proj", "L0_gnn_w1", "L0_gnn_b1", "L0_gnn_w2",
        "L0_gnn_b2", "L0_gnn_g1", "L0_gnn_be1", "L0_gnn_g2", "L0_gnn_be2", "L1_gnn_Wt", "L1_gnn_bt",
        "L1_gnn_Wa", "L1_gnn_ba", "L1_gnn_Wp", "L1_gnn_bp", "L1_gnn_gamma", "L1_gnn_beta"]


def kernel(**inputs):
    import numpy as np
    import concourse.bacc as bacc
    from concourse.bass_utils import run_bass_kernel_spmd

    nc = bacc.Bacc("TRN2", target_bir_lowering=False, num_devices=1)
    arrays = {f"in_{name}": np.ascontiguousarray(inputs[name]) for name in _INS}
    args = [nc.dram_tensor(name, a.shape, mybir.dt.from_np(a.dtype), kind="ExternalInput").ap()
            for name, a in arrays.items()]
    out = nc.dram_tensor("out_0", arrays["in_x"].shape, F32, kind="ExternalOutput").ap()
    gnn_kernel(nc, *args, out)
    return run_bass_kernel_spmd(nc, [arrays], core_ids=[0]).results[0]["out_0"]
```
